# Optimizing a Trainium2 kernel written in Bass

```python
import numpy as np
import jax
import jax.numpy as jnp

def _softmax(x, axis=-1):
    return jax.nn.softmax(x, axis=axis)

def _gelu(x):
    return jax.nn.gelu(x, approximate=True)

def _silu(x):
    return jax.nn.silu(x)

def _sigmoid(x):
    return jax.nn.sigmoid(x)

def _layernorm(x, axis=-1, eps=1e-05):
    m = jnp.mean(x, axis=axis, keepdims=True)
    v = jnp.var(x, axis=axis, keepdims=True)
    return (x - m) / jnp.sqrt(v + eps)

def _scatter_add(tgt, idx, src, axis=0):
    return tgt.at[idx].add(src)

def _segment_sum(src, seg, n):
    return jax.ops.segment_sum(src, seg, n)
kernel_name = 'mk_gps_d1_gnn_r8_1d8c5e'

def setup_inputs(seed: int=0):
    np.random.seed(seed)
    _w = jnp.asarray

    def _rec_inputs():
        import jax
        import jax.numpy as jnp
        _gk = jax.random.key(seed)
        x = -0.0003019 + 1 * jax.random.normal(jax.random.fold_in(_gk, 1), (2500, 1024), jnp.float32)
        _s = jax.random.randint(jax.random.fold_in(_gk, 2), (20000,), 0, 2500, jnp.int32)
        _d = jax.random.randint(jax.random.fold_in(_gk, 3), (20000,), 0, 2500, jnp.int32)
        _loop = jnp.arange(2500, dtype=jnp.int32)
        src = jnp.concatenate([_s, _d, _loop])
        dst = jnp.concatenate([_d, _s, _loop])
        _o = jnp.argsort(dst, stable=True)
        src = src[_o]
        dst = dst[_o]
        edge_weight = jax.random.uniform(jax.random.fold_in(_gk, 12), (42500,), jnp.float32, 0.0, 0.999998)
        return (x, src, dst, edge_weight)
    x, src, dst, edge_weight = _rec_inputs()

    def _L0_gnn_setup():
        import jax, jax.numpy as jnp
        import numpy as np
        N_NODES = 2500
        N_EDGES = 40000
        F_IN = 1024
        F_OUT = 1024
        key = jax.random.key(seed)
        k1, k2, k3, k4, k5 = jax.random.split(key, 5)
        x = jax.random.normal(k1, (N_NODES, F_IN), dtype=jnp.float32)
        std = 1.0 / np.sqrt(F_OUT)
        W = jax.random.uniform(k2, (F_IN, F_OUT), minval=-std, maxval=std, dtype=jnp.float32)
        edge_w = jax.random.uniform(k3, (N_EDGES,), dtype=jnp.float32)
        src = jax.random.randint(k4, (N_EDGES,), 0, N_NODES, dtype=jnp.int32)
        dst = jax.random.randint(k5, (N_EDGES,), 0, N_NODES, dtype=jnp.int32)
        return {'x': x, 'W': W, 'edge_w': edge_w, 'src': src, 'dst': dst}
    _L0_gnn_all = _L0_gnn_setup()
    _L0_gnn_in = {k: v for k, v in _L0_gnn_all.items() if k in ('W',)}
    del _L0_gnn_all

    def _L0_mix_setup():
        import jax, jax.numpy as jnp
        import numpy as np
        EMBED = 1024
        HEADS = 16
        HEAD_DIM = EMBED // HEADS
        MAP_DIM = HEAD_DIM
        B, S = (2, 512)
        key = jax.random.key(seed)
        ks = jax.random.split(key, 8)
        x = jax.random.normal(ks[0], (B, S, EMBED), jnp.float32)
        scale = 1.0 / np.sqrt(EMBED)
        Wq = jax.random.normal(ks[1], (EMBED, EMBED), jnp.float32) * scale
        Wk = jax.random.normal(ks[2], (EMBED, EMBED), jnp.float32) * scale
        Wv = jax.random.normal(ks[3], (EMBED, EMBED), jnp.float32) * scale
        bq = jax.random.normal(ks[4], (EMBED,), jnp.float32) * 0.01
        bk = jax.random.normal(ks[5], (EMBED,), jnp.float32) * 0.01
        bv = jax.random.normal(ks[6], (EMBED,), jnp.float32) * 0.01
        weights = jax.random.normal(ks[7], (HEADS, MAP_DIM, HEAD_DIM), jnp.float32)
        return {'x': x, 'Wq': Wq, 'bq': bq, 'Wk': Wk, 'bk': bk, 'Wv': Wv, 'bv': bv, 'weights': weights}
    _L0_mix_all = _L0_mix_setup()
    _L0_mix_in = {k: v for k, v in _L0_mix_all.items() if k in ('Wq', 'bq', 'Wk', 'bk', 'Wv', 'bv', 'weights')}
    del _L0_mix_all

    def _L0_ffn_setup():
        import jax, jax.numpy as jnp
        import numpy as np
        HIDDEN = 1024
        INNER = 512

        def _weight_quant(w):
            scale = 1.0 / jnp.clip(jnp.mean(jnp.abs(w)), 1e-05)
            wq = jnp.clip(jnp.round(w * scale), -1.0, 1.0) / scale
            return w + jax.lax.stop_gradient(wq - w)

        def _act_quant(x):
            scale = 127.0 / jnp.clip(jnp.max(jnp.abs(x), axis=-1, keepdims=True), 1e-05)
            xq = jnp.clip(jnp.round(x * scale), -128.0, 127.0) / scale
            return x + jax.lax.stop_gradient(xq - x)

        def _bitlinear(x, w):
            return jnp.einsum('bsi,oi->bso', _act_quant(x), _weight_quant(w))
        key = jax.random.key(seed)
        k0, k1, k2, k3 = jax.random.split(key, 4)
        x = jax.random.normal(k0, (4, 256, HIDDEN), dtype=jnp.float32)
        w_gate = jax.random.normal(k1, (INNER, HIDDEN), dtype=jnp.float32) / np.sqrt(HIDDEN)
        w_up = jax.random.normal(k2, (INNER, HIDDEN), dtype=jnp.float32) / np.sqrt(HIDDEN)
        w_down = jax.random.normal(k3, (HIDDEN, INNER), dtype=jnp.float32) / np.sqrt(INNER)
        return {'x': x, 'w_gate': w_gate, 'w_up': w_up, 'w_down': w_down}
    _L0_ffn_all = _L0_ffn_setup()
    _L0_ffn_in = {k: v for k, v in _L0_ffn_all.items() if k in ('w_gate', 'w_up', 'w_down')}
    del _L0_ffn_all
    return {'x': x, 'src': src, 'dst': dst, 'edge_weight': edge_weight, 'L0_gnn_W': _L0_gnn_in['W'], 'L0_mix_Wq': _L0_mix_in['Wq'], 'L0_mix_bq': _L0_mix_in['bq'], 'L0_mix_Wk': _L0_mix_in['Wk'], 'L0_mix_bk': _L0_mix_in['bk'], 'L0_mix_Wv': _L0_mix_in['Wv'], 'L0_mix_bv': _L0_mix_in['bv'], 'L0_mix_weights': _L0_mix_in['weights'], 'L0_ffn_w_gate': _L0_ffn_in['w_gate'], 'L0_ffn_w_up': _L0_ffn_in['w_up'], 'L0_ffn_w_down': _L0_ffn_in['w_down']}

def reference(x, src, dst, edge_weight, L0_gnn_W, L0_mix_Wq, L0_mix_bq, L0_mix_Wk, L0_mix_bk, L0_mix_Wv, L0_mix_bv, L0_mix_weights, L0_ffn_w_gate, L0_ffn_w_up, L0_ffn_w_down):
    import jax
    import jax.numpy as jnp

    def _L0_gnn_ref(x, W, edge_w, src, dst):
        import jax, jax.numpy as jnp
        import numpy as np
        N_NODES = 2500
        N_EDGES = 40000
        F_IN = 1024
        F_OUT = 1024
        support = jnp.matmul(x, W)
        messages = support[src] * edge_w[:, None]
        out = jax.ops.segment_sum(messages, dst, num_segments=N_NODES)
        return out

    def _L0_mix_ref(x, Wq, bq, Wk, bk, Wv, bv, weights):
        import jax, jax.numpy as jnp
        import numpy as np
        EMBED = 1024
        HEADS = 16
        HEAD_DIM = EMBED // HEADS
        MAP_DIM = HEAD_DIM
        B, S = (2, 512)
        Bx, Sx, E = x.shape
        H, M, D = weights.shape
        q = (x @ Wq.T + bq).reshape(Bx, Sx, H, D)
        k = (x @ Wk.T + bk).reshape(Bx, Sx, H, D)
        v = (x @ Wv.T + bv).reshape(Bx, Sx, H, D)
        q = q / jnp.linalg.norm(q)
        k = k / jnp.linalg.norm(k)

        def phi(t):
            sq_norm = jnp.sum(t * t)
            scale = jnp.exp(-sq_norm / 2) / jnp.sqrt(jnp.float32(M))
            return jnp.exp(jnp.einsum('hmd,bshd->bshm', weights, t)) * scale
        phi_q = phi(q)
        phi_k = phi(k)
        s = jnp.einsum('bshm,bshm->bsh', phi_q, phi_k)[..., None]
        out = s * v / s
        return out.reshape(Bx, Sx, E)

    def _L0_ffn_ref(x, w_gate, w_up, w_down):
        import jax, jax.numpy as jnp
        import numpy as np
        HIDDEN = 1024
        INNER = 512

        def _weight_quant(w):
            scale = 1.0 / jnp.clip(jnp.mean(jnp.abs(w)), 1e-05)
            wq = jnp.clip(jnp.round(w * scale), -1.0, 1.0) / scale
            return w + jax.lax.stop_gradient(wq - w)

        def _act_quant(x):
            scale = 127.0 / jnp.clip(jnp.max(jnp.abs(x), axis=-1, keepdims=True), 1e-05)
            xq = jnp.clip(jnp.round(x * scale), -128.0, 127.0) / scale
            return x + jax.lax.stop_gradient(xq - x)

        def _bitlinear(x, w):
            return jnp.einsum('bsi,oi->bso', _act_quant(x), _weight_quant(w))
        gate = jax.nn.silu(_bitlinear(x, w_gate))
        up = _bitlinear(x, w_up)
        return _bitlinear(gate * up, w_down)
    xn = _layernorm(x, axis=-1)
    x = x + _L0_gnn_ref(xn, L0_gnn_W, edge_weight, src, dst) + _L0_mix_ref(xn[None], L0_mix_Wq, L0_mix_bq, L0_mix_Wk, L0_mix_bk, L0_mix_Wv, L0_mix_bv, L0_mix_weights)[0]
    x = x + _L0_ffn_ref(_layernorm(x, axis=-1)[None], L0_ffn_w_gate, L0_ffn_w_up, L0_ffn_w_down)[0]
    return x

_drawn_inputs = setup_inputs


def setup_inputs(seed=0):
    import zlib

    import numpy as np

    out = dict(_drawn_inputs(seed))
    spreads = {}
    factors = {'L0_mix_Wq': 8.0,
     'L0_mix_bq': 8.0,
     'L0_mix_Wk': 8.0,
     'L0_mix_bk': 8.0,
     'L0_mix_bv': 8.0,
     'L0_mix_weights': 8.0}
    for name, (base, spread) in spreads.items():
        noise = np.random.default_rng([zlib.crc32(name.encode()), seed]).standard_normal(out[name].shape)
        drawn = base * np.exp(spread * noise) if base else spread * noise
        out[name] = jnp.asarray(drawn.astype(out[name].dtype))
    for name, factor in factors.items():
        out[name] = (out[name] * factor).astype(out[name].dtype)
    return out
```

```python
import numpy as np

import concourse.bass as bass
from concourse import mybir

F32 = mybir.dt.float32
F32R = mybir.dt.float32r
BF16 = mybir.dt.bfloat16
I32 = mybir.dt.int32
U32 = mybir.dt.uint32
ALU = mybir.AluOpType
ACT = mybir.ActivationFunctionType
AX = mybir.AxisListType

P = 128
NODES = 2500
EDGES = 42500
D = 1024
KT = D // P
INNER = 512
HEADS = 16
HD = D // HEADS
ROWS = 125
TILES = NODES // ROWS
GT = 4
GN = GT * ROWS
GROUPS = TILES // GT
LN_EPS = 1e-5
QUANT_EPS = 1e-5
ROUND = 1.5 * 2.0 ** 23

A_PITCH = 2560
CH_BLOCK = 8
PAIRS = CH_BLOCK // 2
FULL = EDGES // P
TAIL = EDGES - FULL * P
AHEAD = 2
PER_IT = 4
ITERS = 2 * GROUPS
BLOCKS = AHEAD + PER_IT * ITERS
CHUNKS = BLOCKS * CH_BLOCK
ROWS_C = CHUNKS + 2 * CH_BLOCK
assert CHUNKS * P >= EDGES
CT = ROWS_C // 4

SBUF_AT = 16640
SMALL_AT = SBUF_AT
KEYS_AT = SMALL_AT + 5120
W_AT = KEYS_AT + 5 * 4 * ROWS_C
S_AT = W_AT + 2 * 4 * KT * D
E_AT = S_AT + 4 * TILES * D
END_AT = 229368


def split_rows(eng, dst, src, sem):
    cut = 112
    eng.dma_start(dst[0:cut], src[0:cut]).then_inc(sem, 16)
    eng.dma_start(dst[cut:ROWS], src[cut:ROWS]).then_inc(sem, 16)


def layer_kernel(nc, x, src, dst, edge_weight, W, Wq, bq, Wk, bk, Wv, bv, mix_w, w_gate, w_up, w_down, out):
    A = nc.dram_tensor("A_dense", (A_PITCH, A_PITCH), F32).ap()
    key_d = nc.dram_tensor("key_rows", (ROWS_C, P), F32).ap()
    ew_d = nc.dram_tensor("weight_rows", (ROWS_C, P), F32).ap()
    xnT_d = nc.dram_tensor("xnT", (TILES, P, KT, ROWS), F32).ap()
    uT_d = nc.dram_tensor("uT", (2, P, KT, NODES), F32).ap()
    z_d = nc.dram_tensor("z", (NODES, D), F32).ap()
    r_d = nc.dram_tensor("r", (NODES, D), F32).ap()

    cursor = {}

    def zone(label, at, end):
        cursor[label] = at

        def put(name, shape, dt=F32):
            size = 2 if dt == BF16 else 4
            here = cursor[label]
            cursor[label] = here + (int(np.prod(shape[1:])) * size + 31) // 32 * 32
            assert cursor[label] <= end, (name, cursor[label], end)
            return nc.alloc_sbuf_tensor_at(name, shape, dt, offset=here)
        return put

    small = zone("small", SMALL_AT, KEYS_AT)
    ident = small("ident", [P, P])
    ident16 = small("ident16", [P, P], BF16)
    ones = small("ones", [P, P])
    earlier = small("earlier", [P, 2, P])
    sel = small("sel", [P, 2])
    eps = small("eps", [P, 1])
    neg_round = small("neg_round", [P, 1])
    bqk = small("bqk", [P, 2, KT])
    mv = small("mv", [P, TILES, 2])
    std = small("std", [P, TILES])
    rstd = small("rstd", [P, TILES])
    stats = small("stats", [P, GT, 2, 6])
    group_mv = small("group_mv", [P, GT, 2])
    ssq = small("ssq", [P, 2 * GROUPS * KT])
    norms = small("norms", [P, 8, 2])
    s_sb = small("s_sb", [P, 2, HEADS])
    rs_sb = small("rs_sb", [P, 2, HEADS])
    w_slot = small("w_slot", [P, 2, CH_BLOCK])
    to_dummy = small("to_dummy", [P, 2, CH_BLOCK])
    cell_slot = small("cell_slot", [P, 2, CH_BLOCK], U32)
    wabs = small("wabs", [P, 16])
    wsum = small("wsum", [P, 4])
    wq_sc = small("wq_sc", [P, 4, 4])
    x_sc = small("x_sc", [P, 2, 4])
    h_sc = small("h_sc", [P, 2, 4])

    keys = zone("keys", KEYS_AT, W_AT)
    key = keys("key", [P, ROWS_C])
    ew = keys("ew", [P, ROWS_C])
    away = keys("away", [P, ROWS_C])
    wtot = keys("wtot", [P, ROWS_C])
    dup = keys("dup", [P, ROWS_C])

    wz = zone("W", W_AT, S_AT)
    WH = wz("WH", [P, KT, D], F32R)
    WL = wz("WL", [P, KT, D], F32R)
    w1 = zone("W1", W_AT, S_AT)
    XT = w1("XT", [P, 2, KT, ROWS])
    iedge = w1("iedge", [P, 2, ROWS_C], I32)
    kT_sb = w1("kT_sb", [P, 8, P])

    X = zone("S1", S_AT, E_AT)("X", [P, TILES, D])
    s2 = zone("S2", S_AT, E_AT)
    xgH = s2("xgH", [P, 2, KT, GN], F32R)
    xgL = s2("xgL", [P, 2, KT, GN], F32R)
    xg = s2("xg", [P, GT, KT, ROWS])
    S = zone("S3", S_AT, E_AT)("S", [P, TILES, D])

    e1 = zone("E1", E_AT, END_AT)
    wst = e1("wst", [P, 2, D])
    keyrow = e1("keyrow", [P, 2, CH_BLOCK * P])
    ewrow = e1("ewrow", [P, 2, CH_BLOCK * P])
    junk = e1("junk", [P, 2, 7, P], BF16)
    zeros = e1("zeros", [P, A_PITCH // 4])
    bdH = e1("bdH", [P, KT, P], F32R)
    bdL = e1("bdL", [P, KT, P], F32R)
    at = cursor["E1"]
    XN = zone("E1a", at, END_AT)("XN", [P, 2, D])
    e1b = zone("E1b", at, END_AT)
    qH = e1b("qH", [P, 2, GN], F32R)
    qL = e1b("qL", [P, 2, GN], F32R)
    usb = e1b("usb", [P, 2, GN])
    squares = e1b("squares", [P, 2, GN], BF16)

    e2 = zone("E2", E_AT, END_AT)
    xt = e2("xt", [P, 2, KT, ROWS])
    xtH = [e2(f"xtH{i}", [P, KT, ROWS], F32R) for i in range(2)]
    xtL = [e2(f"xtL{i}", [P, KT, ROWS], F32R) for i in range(2)]
    bvb = e2("bvb", [P, D])
    at = cursor["E2"]
    wst2 = zone("E2a", at, END_AT)("wst2", [P, 2, D])
    e2b = zone("E2b", at, END_AT)
    ut = e2b("ut", [P, 2, 2, KT, ROWS])
    zx = e2b("zx", [P, 2, D])

    w3 = zone("W3", W_AT, S_AT)
    wgT = w3("wgT", [P, KT, INNER], BF16)
    wuT = w3("wuT", [P, KT, INNER], BF16)
    wdT = w3("wdT", [P, INNER // P, D], BF16)
    Araw = w3("Araw", [P, 2, GN])
    AH = [w3(f"AH{i}", [P, GN], F32R) for i in range(2)]
    AL = [w3(f"AL{i}", [P, GN], F32R) for i in range(2)]
    SH = w3("SH", [P, 2, D], F32R)
    SL = w3("SL", [P, 2, D], F32R)
    zr = zone("E3", E_AT, END_AT)("zr", [P, GT, D])

    s6 = zone("S6", S_AT, E_AT)
    fw = [s6(f"fw{f}", [P, 4, D]) for f in range(3)]
    fq = [s6(f"fq{f}", [P, 4, D], BF16) for f in range(3)]
    e6 = zone("E6", E_AT, END_AT)
    rt = e6("rt", [P, 2, D])
    rc = e6("rc", [P, 2, D])
    rq16 = e6("rq16", [P, 2, D], BF16)
    rqT = e6("rqT", [P, 2, KT, P], BF16)
    gate = e6("gate", [P, 2, INNER])
    hid = e6("hid", [P, 2, INNER])
    hq16 = e6("hq16", [P, 2, INNER], BF16)
    hqT = e6("hqT", [P, 2, INNER // P, P], BF16)
    fin = e6("fin", [P, 2, D])

    PS = nc.alloc_psum_tensor("PS", [P, 8, 512], F32)
    PS16 = PS[:, :, :].bitcast(BF16)

    def two_banks(slot):
        return PS[:, 2 * slot:2 * slot + 2, :].rearrange("p b n -> p (b n)")

    def by_block(ap):
        return ap.rearrange("p (k n) -> p k n", k=KT)

    def sem(name):
        return nc.alloc_semaphore(name)

    def sems(name, n=2):
        return [sem(f"{name}{i}") for i in range(n)]

    HALF = TILES // 2
    Q_BLOCKS = ITERS * KT // 2
    ZX_END = 32 * (HALF + 1)
    s_Ar = sems("s_Ar", 2)
    s_Azero = sem("s_Azero")
    s_acc = sems("s_acc", GT)
    s_bd = sem("s_bd")
    s_bdh = sem("s_bdh")
    s_bdl = sem("s_bdl")
    s_bdtr = sem("s_bdtr")
    s_bdz = sem("s_bdz")
    s_bias = sem("s_bias")
    s_bv = sem("s_bv")
    s_const = sem("s_const")
    s_edges = sem("s_edges")
    s_ew = sem("s_ew")
    s_exp = sems("s_exp", 2)
    s_f6 = sem("s_f6")
    s_fT = sems("s_fT", 2)
    s_fabs = sem("s_fabs")
    s_fc = sem("s_fc")
    s_fill = sem("s_fill")
    s_flags = sem("s_flags")
    s_fs = sem("s_fs")
    s_ftot = sem("s_ftot")
    s_ftr = sems("s_ftr", 2)
    s_fw = sems("s_fw", 3)
    s_go = sem("s_go")
    s_go2 = sem("s_go2")
    s_gate = sems("s_gate", 2)
    s_h = sems("s_h", 2)
    s_h6 = sem("s_h6")
    s_hi5 = sems("s_hi5", 2)
    s_hq = sems("s_hq", 2)
    s_hq16 = sems("s_hq16", 2)
    s_id16 = sem("s_id16")
    s_key = sem("s_key")
    s_kout = sem("s_kout")
    s_ksb = sem("s_ksb")
    s_ktr = sem("s_ktr")
    s_lo5 = sems("s_lo5", 2)
    s_mm = sems("s_mm", 2)
    s_n = sems("s_n", 8)
    s_pad = sem("s_pad")
    s_pair = sems("s_pair", 2)
    s_pe5 = sems("s_pe5", 2)
    s_phi = sems("s_phi", 2)
    s_q = sems("s_q", 2)
    s_ql = sems("s_ql", 2)
    s_r = sems("s_r", GT)
    s_rag = sem("s_rag")
    s_rmv = sem("s_rmv")
    s_rout = sem("s_rout")
    s_row = sems("s_row", 2)
    s_rq = sems("s_rq", 2)
    s_rq16 = sems("s_rq16", 2)
    s_rqT = sems("s_rqT", 2)
    s_rst = sem("s_rst")
    s_rstd = sem("s_rstd")
    s_rtr = sems("s_rtr", 2)
    s_s = sems("s_s", 2)
    s_sc = sems("s_sc", 2)
    s_slot = sem("s_slot")
    s_sq = sems("s_sq", 2)
    s_st = sem("s_st")
    s_stc = sem("s_stc")
    s_std = sem("s_std")
    s_supev = sems("s_supev", 2)
    s_u = sems("s_u", 2)
    s_uev = sems("s_uev", 2)
    s_uout = sems("s_uout", 2)
    s_ut = sems("s_ut", 2)
    s_vc = sem("s_vc")
    s_w2h = sem("s_w2h")
    s_w2l = sem("s_w2l")
    s_wh = sems("s_wh", 2)
    s_wl = sems("s_wl", 2)
    s_wst = sems("s_wst", 2)
    s_wtr = sems("s_wtr", 2)
    s_x = sems("s_x", GROUPS)
    s_xev = sems("s_xev", 2)
    s_xg = sem("s_xg")
    s_xgh = sem("s_xgh")
    s_xgl = sem("s_xgl")
    s_xn = sems("s_xn", 2)
    s_xout = sems("s_xout", 2)
    s_xt = sems("s_xt", 2)
    s_xth = sems("s_xth", 2)
    s_xtl = sems("s_xtl", 2)
    s_xtr = sems("s_xtr", 2)
    s_z = sems("s_z", 2)
    s_zin = sem("s_zin")
    s_zx = sems("s_zx", 2)

    def product3(o, lh, ll, rh, rl, start, stop):
        nc.tensor.matmul(o, lh, rl, start=start, stop=False)
        nc.tensor.matmul(o, ll, rh, start=False, stop=False)
        return nc.tensor.matmul(o, lh, rh, start=False, stop=stop)

    def edge_pair(dve, pair, uses, block_slot, i):
        slot = i % 2
        row, wrow = (b[:, block_slot, 2 * i * P:(2 * i + 2) * P] for b in (keyrow, ewrow))
        dve.wait_ge(s_pair[slot], uses)
        for c in range(2):
            col = bass.ds(pair * 2 + c, 1)
            nc.vector.scalar_tensor_tensor(junk[:, slot, 2 * c:2 * c + 2, :].rearrange("p a n -> p (a n)"), row,
                                           key[:, col], wrow, ALU.is_equal, ALU.mult, accum_out=wtot[:, col])
        nc.vector.scalar_tensor_tensor(junk[:, slot, 4, :], row[:, 0:P], key[:, bass.ds(pair * 2, 1)],
                                       earlier[:, 1, :], ALU.is_equal, ALU.mult,
                                       accum_out=dup[:, bass.ds(pair * 2, 1)])
        nc.vector.scalar_tensor_tensor(junk[:, slot, 5:7, :].rearrange("p a n -> p (a n)"), row,
                                       key[:, bass.ds(pair * 2 + 1, 1)],
                                       earlier[:, :, :].rearrange("p a n -> p (a n)"), ALU.is_equal, ALU.mult,
                                       accum_out=dup[:, bass.ds(pair * 2 + 1, 1)]).then_inc(s_pair[slot], 1)

    def edge_flags(dve, b):
        for k in range(2):
            dve.wait_ge(s_pair[k], (b + 1) * (PAIRS // 2))
        cols = bass.ds(b * CH_BLOCK, CH_BLOCK)
        nc.vector.tensor_scalar(dup[:, cols], dup[:, cols], 1.0, None, ALU.min).then_inc(s_flags, 1)

    block_cm = nc.Block()
    block = block_cm.__enter__()

    @block.sync
    def _(sp):
        for i, v in enumerate((src, dst)):
            sp.dma_start(iedge[:, i, 0:FULL], v[0:FULL * P].rearrange("(p c) -> p c", p=P)).then_inc(s_edges, 16)
            sp.dma_start(iedge[0:TAIL, i, FULL:FULL + 1],
                         v[FULL * P:EDGES].rearrange("(p c) -> p c", c=1)).then_inc(s_edges, 16)
        sp.wait_ge(s_fill, 3)
        sp.dma_start(ew[:, 0:FULL], edge_weight[0:FULL * P].rearrange("(p c) -> p c", p=P)).then_inc(s_ew, 16)
        sp.dma_start(ew[0:TAIL, FULL:FULL + 1],
                     edge_weight[FULL * P:EDGES].rearrange("(p c) -> p c", c=1)).then_inc(s_ew, 16)
        sp.wait_ge(s_bdz, 1)
        mw = mix_w.rearrange("(j h) m d -> h m j d", h=2)
        for h in range(2):
            sp.dma_start(by_block(wst[:, 0, :])[h * HD:(h + 1) * HD, :, h * HD:(h + 1) * HD], mw[h]).then_inc(s_bd, 16)
        for g in range(GROUPS):
            split_rows(sp, X[:, g * GT:(g + 1) * GT, :],
                       x[g * GN:(g + 1) * GN, :].rearrange("(t r) d -> r t d", r=ROWS), s_x[g])
        with nc.allow_non_contiguous_dma(reason="two vectors of biases"):
            for i, v in enumerate((bq, bk)):
                sp.dma_start(bqk[:, i, :], v.rearrange("(j p) -> p j", p=P)).then_inc(s_bias, 16)
        sp.wait_ge(s_ksb, 2)
        for q, dram in ((0, key_d), (1, ew_d)):
            sp.dma_start(dram.rearrange("(b c) p -> c b p", c=CT), kT_sb[0:CT, 4 * q:4 * q + 4, :]).then_inc(s_kout, 16)
        sp.wait_ge(s_kout, 32)

        def load_key_rows(b, slot):
            for buf, dram in ((keyrow, key_d), (ewrow, ew_d)):
                sp.dma_start(buf[:, slot, :], dram[bass.ds(b * CH_BLOCK, CH_BLOCK), :].rearrange("(o c) p -> o (c p)", o=1)
                             .to_broadcast([P, CH_BLOCK * P])).then_inc(s_row[slot], 16)

        for b in range(AHEAD):
            load_key_rows(b, b)
        with sp.Fori(0, TILES // 2) as h:
            for i in range(2):
                sp.wait_ge(s_xev[i], h + 1)
                sp.dma_start(xnT_d[bass.ds(h * 2 + i, 1)].rearrange("o p k r -> (o p) (k r)"),
                             XT[:, i].rearrange("p k r -> p (k r)")).then_inc(s_xout[i], 16)
        for i in range(2):
            sp.wait_ge(s_xout[i], 16 * TILES // 2)
        def load_group(g):
            sp.dma_start(xg[:, :, :, :].rearrange("p t k r -> p t (k r)"),
                         xnT_d[bass.ds(g * GT, GT)].rearrange("t p k r -> p t (k r)")).then_inc(s_xg, 16)

        load_group(0)
        for b in range(AHEAD):
            for k in range(2):
                sp.wait_ge(s_pair[k], (b + 1) * (PAIRS // 2))
            load_key_rows(b + AHEAD, b)

        for mat, w in enumerate((Wq, Wk)):
            for j in range(KT):
                m = mat * (KT // 2) + j // 2
                if m:
                    sp.wait_ge(s_wtr[j % 2], m)
                elif j == 0:
                    sp.wait_ge(s_bdtr, 1)
                sp.dma_start(wst[:, j % 2, :], w[j * P:(j + 1) * P, :]).then_inc(s_wst[j % 2], 16)
            with sp.Fori(0, GROUPS) as g:
                it = g + mat * GROUPS
                for hl in (s_xgh, s_xgl):
                    sp.wait_ge(hl, it * GT + GT)
                load_group((g + 1) % GROUPS)
                for j in range(KT):
                    m = it * (KT // 2) + j // 2
                    sp.wait_ge(s_uev[j % 2], m + 1)
                    sp.dma_start(uT_d[mat, :, j, bass.ds(g * GN, GN)], usb[:, j % 2, :]).then_inc(s_uout[j % 2], 16)
                    if j % 2:
                        b = it * PER_IT + AHEAD + j // 2
                        for k in range(2):
                            sp.wait_ge(s_pair[k], (b + 1) * (PAIRS // 2))
                        load_key_rows(b + AHEAD, (j // 2) % 2)
        for i in range(2):
            sp.wait_ge(s_uout[i], 16 * ITERS * KT // 2)
            sp.wait_ge(s_u[i], ITERS * KT // 2)
            sp.wait_ge(s_sq[i], ITERS * KT // 2)
            sp.wait_ge(s_row[i], 32 * (BLOCKS // 2 + 1))
        sp.wait_ge(s_flags, BLOCKS)
        sp.wait_ge(s_Azero, 16 * A_PITCH // P)
        sp.dma_start(bvb[:, :], bv.rearrange("(o n) -> o n", o=1).to_broadcast([P, D])).then_inc(s_bv, 16)
        for k in range(KT):
            if k >= 2:
                sp.wait_ge(s_w2h, k - 1)
                sp.wait_ge(s_w2l, k - 1)
            sp.dma_start(wst2[:, k % 2, :], W[k * P:(k + 1) * P, :]).then_inc(s_wst[k % 2], 16)

        def load_tile(t, i):
            sp.dma_start(xt[:, i].rearrange("p k r -> p (k r)"),
                         xnT_d[bass.ds(t, 1)].rearrange("o p k r -> (o p) (k r)")).then_inc(s_xt[i], 16)

        for i in range(2):
            load_tile(i, i)
        with sp.Fori(0, TILES // 2) as h:
            for i in range(2):
                sp.wait_ge(s_xth[i], h + 1)
                sp.wait_ge(s_xtl[i], h + 1)
                load_tile((h * 2 + i + 2) % TILES, i)
        sp.wait_ge(s_w2h, KT)
        sp.wait_ge(s_w2l, KT)
        for j in range(KT):
            if j >= 2:
                sp.wait_ge(s_wtr[j % 2], KT + j // 2)
            sp.dma_start(wst2[:, j % 2, :], Wv[j * P:(j + 1) * P, :]).then_inc(s_wst[j % 2], 16)
        for i in range(2):
            sp.wait_ge(s_wtr[i], KT + KT // 2)

        def load_u(t, i):
            for m in range(2):
                sp.dma_start(ut[:, i, m], uT_d[m, :, :, bass.ds(t * ROWS, ROWS)]).then_inc(s_ut[i], 16)

        def load_x(t, i):
            split_rows(sp, zx[:, i, :], x[bass.ds(t * ROWS, ROWS), :], s_zx[i])

        for i in range(2):
            load_u(i, i)
            load_x(i, i)
        with sp.Fori(0, TILES // 2) as h:
            for i in range(2):
                t = h * 2 + i
                nxt = (t + 2) % TILES
                sp.wait_ge(s_xth[i], h + TILES // 2 + 1)
                sp.wait_ge(s_xtl[i], h + TILES // 2 + 1)
                load_tile(nxt, i)
                sp.wait_ge(s_s[i], h + 1)
                load_u(nxt, i)
                sp.wait_ge(s_z[i], h + 1)
                split_rows(sp, z_d[bass.ds(t * ROWS, ROWS), :], zx[:, i, :], s_xout[i])
                sp.wait_ge(s_xout[i], 16 * TILES // 2 + h * 32 + 32)
                load_x(nxt, i)
        for i in range(2):
            sp.wait_ge(s_zx[i], 32 * (TILES // 2 + 1))
            sp.wait_ge(s_ut[i], 32 * (TILES // 2 + 1))
            sp.wait_ge(s_xt[i], 16 * (TILES + 1))
            sp.wait_ge(s_mm[i], TILES)
            sp.wait_ge(s_s[i], TILES // 2)
            sp.wait_ge(s_sc[i], 16 * CHUNKS // 2)

        def load_A(s, g, i):
            sp.dma_start(Araw[:, i, :], A[bass.ds(s * ROWS, P), bass.ds(g * GN, GN)]).then_inc(s_Ar[i], 16)

        def load_z(g):
            split_rows(sp, zr[:, :, :], z_d[bass.ds(g * GN, GN), :].rearrange("(t r) d -> r t d", r=ROWS), s_zin)

        load_z(0)
        for i in range(2):
            load_A(i, 0, i)
        half = TILES // 2
        with sp.Fori(0, GROUPS) as g:
            with sp.Fori(0, half - 1) as h:
                for i in range(2):
                    sp.wait_ge(s_hi5[i], g * half + h + 1)
                    sp.wait_ge(s_lo5[i], g * half + h + 1)
                    load_A(h * 2 + i + 2, g, i)
            for i in range(2):
                sp.wait_ge(s_hi5[i], g * half + half)
                sp.wait_ge(s_lo5[i], g * half + half)
                load_A(i, (g + 1) % GROUPS, i)
            sp.wait_ge(s_r[GT - 1], g + 1)
            split_rows(sp, r_d[bass.ds(g * GN, GN), :].rearrange("(t r) d -> r t d", r=ROWS), zr[:, :, :], s_rout)
            sp.wait_ge(s_rout, g * 32 + 32)
            sp.wait_ge(s_rmv, g + 1)
            load_z((g + 1) % GROUPS)
        sp.wait_ge(s_zin, 32 * (GROUPS + 1))
        for i in range(2):
            sp.wait_ge(s_Ar[i], 16 * (GROUPS * half + 1))
            sp.wait_ge(s_hi5[i], GROUPS * half + 1)
            sp.wait_ge(s_lo5[i], GROUPS * half + 1)
        for f, (w, rows) in enumerate(((w_gate, INNER), (w_up, INNER), (w_down, D))):
            sp.dma_start(fw[f][:, :, :].rearrange("p a n -> p (a n)").rearrange("p (a n) -> p a n", a=rows // P),
                         w.rearrange("(a p) n -> p a n", p=P)).then_inc(s_fw[f], 16)

        def load_r(t, i):
            split_rows(sp, rt[:, i, :], r_d[bass.ds(t * ROWS, ROWS), :], s_zx[i])

        for i in range(2):
            load_r(i, i)
        with sp.Fori(0, half) as h:
            for i in range(2):
                t = h * 2 + i
                sp.wait_ge(s_z[i], HALF + h + 1)
                split_rows(sp, out[bass.ds(t * ROWS, ROWS), :], fin[:, i, :], s_uout[i])
                load_r((t + 2) % TILES, i)
        for i in range(2):
            sp.wait_ge(s_zx[i], ZX_END + 32 * (half + 1))
            sp.wait_ge(s_uout[i], Q_BLOCKS * 16 + 32 * half)

    @block.gpsimd
    def _(pool):
        pool.memset(wst[:, 0, :], 0.0).then_inc(s_bdz, 1)
        pool.memset(ew[:, :], 0.0).then_inc(s_fill, 1)
        for t in (key, away):
            pool.iota(t[:, :], [[0, ROWS_C // 2], [1, 2]], base=A_PITCH - 2, channel_multiplier=A_PITCH,
                      allow_small_or_imprecise_dtypes=True).then_inc(s_fill, 1)
        pool.memset(ident[:, :], 0.0).then_inc(s_const, 1)
        pool.memset(earlier[:, :, :], 1.0).then_inc(s_const, 1)
        pool.memset(ones[:, :], 1.0).then_inc(s_const, 1)
        pool.memset(eps[:, :], LN_EPS).then_inc(s_const, 1)
        pool.memset(neg_round[:, :], -ROUND).then_inc(s_const, 1)
        pool.memset(zeros[:, :], 0.0).then_inc(s_const, 1)
        pool.wait_ge(s_const, 6)
        pool.affine_select(out=ident[:, :], in_=ident[:, :], compare_op=ALU.not_equal, fill=1.0, base=0,
                           pattern=[[-1, P]], channel_multiplier=1).then_inc(s_const, 1)
        pool.affine_select(out=earlier[:, 1, :], in_=earlier[:, 1, :], compare_op=ALU.is_gt, fill=0.0, base=0,
                           pattern=[[-1, P]], channel_multiplier=1).then_inc(s_const, 1)
        pool.wait_ge(s_const, 8)
        pool.tensor_copy(ident16[:, :], ident[:, :]).then_inc(s_id16, 1)

        for g in range(GROUPS):
            pool.wait_ge(s_x[g], 32)
        for i in range(A_PITCH // P):
            pool.dma_start(A[i * P:(i + 1) * P, :].rearrange("p (r c) -> p r c", r=4),
                           zeros[:, None, :].to_broadcast([P, 4, A_PITCH // 4])).then_inc(s_Azero, 16)
        pool.wait_ge(s_Azero, 16 * A_PITCH // P)
        cells = A.rearrange("a (b o) -> (a b) o", o=1)
        with pool.Fori(0, BLOCKS // 2) as h:
            for i in range(2):
                b = h * 2 + i
                cols = bass.ds(b * CH_BLOCK, CH_BLOCK)
                pool.wait_ge(s_flags, b + 1)
                pool.tensor_tensor(to_dummy[:, i, :], away[:, cols], dup[:, cols], ALU.mult).then_inc(s_slot, 1)
                pool.tensor_copy(w_slot[:, i, :], wtot[:, cols]).then_inc(s_slot, 1)
                pool.wait_ge(s_slot, b * 4 + 2)
                pool.tensor_tensor(to_dummy[:, i, :], to_dummy[:, i, :], key[:, cols], ALU.add).then_inc(s_slot, 1)
                pool.wait_ge(s_slot, b * 4 + 3)
                pool.sem_inc(s_go, 1)
                pool.tensor_copy(cell_slot[:, i, :], to_dummy[:, i, :]).then_inc(s_slot, 1)
                pool.wait_ge(s_slot, b * 4 + 4)
                for pr in range(PAIRS):
                    for c in range(2):
                        pool.wait_ge(s_sc[c], (b * PAIRS + pr) * 16)
                    pool.sem_inc(s_go, 1)
                    for c in range(2):
                        col = 2 * pr + c
                        pool.indirect_dma_start(cells, bass.IndirectOffsetOnAxis(cell_slot[:, i, col:col + 1], 0),
                                                w_slot[:, i, col:col + 1], None,
                                                compute_op=ALU.add).then_inc(s_sc[c], 16)

    @block.scalar
    def _(act):
        act.wait_ge(s_bdtr, 1)
        nc.scalar.activation(bdH[:, :, :], by_block(two_banks(0)), ACT.Copy).then_inc(s_bdh, 1)
        for q in range(2):
            act.wait_ge(s_ktr, q + 1)
            nc.scalar.activation(kT_sb[0:CT, 4 * q:4 * q + 4, :], PS[0:CT, 4 + q, :].rearrange("p (b n) -> p b n", b=4),
                                 ACT.Copy).then_inc(s_ksb, 1)
        act.wait_ge(s_st, TILES)
        act.wait_ge(s_const, 6)
        nc.scalar.activation(std[0:ROWS, :], mv[0:ROWS, :, 1], ACT.Sqrt, bias=eps[0:ROWS, :]).then_inc(s_std, 1)
        with act.Fori(0, TILES // 2) as h:
            for i in range(2):
                act.wait_ge(s_xtr[i], h + 1)
                act.wait_ge(s_xout[i], h * 16)
                nc.scalar.activation(XT[:, i], by_block(two_banks(i))[:, :, 0:ROWS], ACT.Copy).then_inc(s_xev[i], 1)

        def high_of_group_tile(n_group, t):
            nc.scalar.activation(xgH[:, bass.ds(n_group % 2, 1), :, t * ROWS:(t + 1) * ROWS]
                                 .rearrange("p o k r -> p (o k) r"), xg[:, t], ACT.Copy).then_inc(s_xgh, 1)

        act.wait_ge(s_xg, 16)
        for t in range(GT):
            high_of_group_tile(0, t)
        act.wait_ge(s_bias, 32)
        act.wait_ge(s_kout, 32)
        for mat in range(2):
            for i in range(2):
                act.wait_ge(s_q[i], mat * GROUPS * KT // 2)
            for j in range(KT):
                act.wait_ge(s_wtr[j % 2], mat * (KT // 2) + j // 2 + 1)
                nc.scalar.activation(WH[:, :, j * P:(j + 1) * P], by_block(two_banks(j % 2)), ACT.Copy).then_inc(s_wh[j % 2], 1)
            with act.Fori(0, GROUPS) as g:
                it = g + mat * GROUPS

                def evacuate_u(j):
                    m = it * (KT // 2) + j // 2
                    act.wait_ge(s_u[j % 2], m + 1)
                    act.wait_ge(s_uout[j % 2], m * 16)
                    nc.scalar.activation(usb[:, j % 2, :], PS[:, 6 + j % 2, 0:GN], ACT.Copy).then_inc(s_uev[j % 2], 1)

                for j in range(KT):
                    m = it * (KT // 2) + j // 2
                    act.wait_ge(s_q[j % 2], m + 1)
                    act.wait_ge(s_u[j % 2], m)
                    bias = bqk[:, mat, j:j + 1]
                    nc.scalar.activation(qH[:, j % 2, :], PS[:, 4 + j % 2, 0:GN], ACT.Identity,
                                         bias=bias)
                    nc.scalar.activation(squares[:, j % 2, :], PS[:, 4 + j % 2, 0:GN], ACT.Square, bias=bias,
                                         accum_out=ssq[:, bass.ds(it * KT + j, 1)]).then_inc(s_sq[j % 2], 1)
                    if j:
                        evacuate_u(j - 1)
                    if j == 0:
                        act.wait_ge(s_xg, it * 16 + 32)
                    if j < GT:
                        high_of_group_tile(it + 1, j)
                evacuate_u(KT - 1)
        act.wait_ge(s_n[1], 1)
        nc.scalar.activation(norms[:, 1, :], PS[:, 0, 0:2], ACT.Sqrt).then_inc(s_n[2], 1)
        act.wait_ge(s_n[4], 2)
        nc.scalar.activation(norms[:, 4, :], norms[:, 3, :], ACT.Exp, scale=-0.5).then_inc(s_n[5], 1)
        for k in range(KT):
            act.wait_ge(s_wst[k % 2], 16 * (KT + k // 2 + 1))
            nc.scalar.activation(WH[:, k, :], wst2[:, k % 2, :], ACT.Copy).then_inc(s_w2h, 1)

        def high_of_tile(i, m):
            act.wait_ge(s_xt[i], m * 16 + 16)
            act.wait_ge(s_mm[i], m)
            nc.scalar.activation(xtH[i][:, :, :], xt[:, i], ACT.Copy).then_inc(s_xth[i], 1)

        high_of_tile(0, 0)
        with act.Fori(0, TILES // 2) as h:
            for i in range(2):
                high_of_tile(1 - i, h + i)
                act.wait_ge(s_mm[i], h + 1)
                nc.scalar.activation(S[0:ROWS, bass.ds(h * 2 + i, 1), :].rearrange("p o n -> p (o n)"),
                                     two_banks(i)[0:ROWS], ACT.Copy).then_inc(s_supev[i], 1)
        for j in range(KT):
            act.wait_ge(s_wtr[j % 2], KT + j // 2 + 1)
            nc.scalar.activation(WH[:, :, j * P:(j + 1) * P], by_block(two_banks(j % 2)), ACT.Copy).then_inc(s_wh[j % 2], 1)
        act.wait_ge(s_n[3], 1)
        with act.Fori(0, TILES // 2) as h:
            for i in range(2):
                high_of_tile(1 - i, h + TILES // 2 + i)
                act.wait_ge(s_ut[i], h * 32 + 32)
                for m in range(2):
                    nc.scalar.activation(ut[:, i, m], ut[:, i, m], ACT.Exp, scale=norms[:, 2, m:m + 1]).then_inc(s_exp[i], 1)
        half = TILES // 2

        def high_of_sources(s, i, m):
            act.wait_ge(s_Ar[i], m * 16 + 16)
            act.wait_ge(s_pe5[i], m)
            nc.scalar.activation(AH[i][0:ROWS, :], Araw[0:ROWS, i, :], ACT.Copy)
            nc.scalar.activation(SH[0:ROWS, i, :], S[0:ROWS, bass.ds(s, 1), :].rearrange("p o n -> p (o n)"),
                                 ACT.Copy).then_inc(s_hi5[i], 1)

        for i in range(2):
            high_of_sources(i, i, 0)
        with act.Fori(0, GROUPS) as g:
            with act.Fori(0, half - 1) as h:
                for i in range(2):
                    high_of_sources(h * 2 + 2 + i, i, g * half + h + 1)
            for i in range(2):
                high_of_sources(i, i, g * half + half)
        act.wait_ge(s_rmv, GROUPS)
        nc.scalar.activation(std[0:ROWS, :], mv[0:ROWS, :, 1], ACT.Sqrt, bias=eps[0:ROWS, :]).then_inc(s_std, 1)
        for f in range(3):
            act.wait_ge(s_fw[f], 16)
            for a in range(4):
                nc.scalar.activation(fq[f][:, a, :], fw[f][:, a, :], ACT.Abs,
                                     accum_out=wabs[:, 4 * f + a:4 * f + a + 1]).then_inc(s_fabs, 1)
        for f, (wT, n) in enumerate(((wgT, KT), (wuT, KT), (wdT, 4))):
            for c in range(4):
                act.wait_ge(s_ftr[c % 2], 2 * f + c // 2 + 1)
                blocks = wT[:, :, :].rearrange("p a n -> p (a n)")[:, c * 1024:(c + 1) * 1024]
                nc.scalar.activation(blocks, PS16[:, c % 2, :], ACT.Copy).then_inc(s_fT[c % 2], 1)

        def integers_x(i, m):
            act.wait_ge(s_rq[i], m + 1)
            act.wait_ge(s_rtr[i], m)
            nc.scalar.activation(rq16[0:ROWS, i, :], rc[0:ROWS, i, :], ACT.Identity,
                                 bias=neg_round[0:ROWS, :]).then_inc(s_rq16[i], 1)

        def transposed_x(i, m):
            act.wait_ge(s_rtr[i], m + 1)
            act.wait_ge(s_q[i], Q_BLOCKS + m)
            nc.scalar.activation(rqT[:, i, :, 0:ROWS], PS16[:, 6, :].rearrange("p (k n) -> p k n", k=KT)[:, :, 0:ROWS],
                                 ACT.Copy).then_inc(s_rqT[i], 1)

        def silu_gate(i, m):
            act.wait_ge(s_q[i], Q_BLOCKS + m + 1)
            act.wait_ge(s_h[i], m)
            nc.scalar.activation(gate[0:ROWS, i, :], PS[0:ROWS, 2 * i, :], ACT.Silu,
                                 scale=x_sc[0:ROWS, i, 2:3]).then_inc(s_gate[i], 1)

        for i in range(2):
            integers_x(i, 0)
            transposed_x(i, 0)
            if i == 0:
                silu_gate(0, 0)
        with act.Fori(0, half) as h:
            for i in range(2):
                act.wait_ge(s_hq[i], h + 1)
                act.wait_ge(s_xtr[i], HALF + h)
                nc.scalar.activation(hq16[0:ROWS, i, :], hid[0:ROWS, i, :], ACT.Identity,
                                     bias=neg_round[0:ROWS, :]).then_inc(s_hq16[i], 1)
                act.wait_ge(s_xtr[i], HALF + h + 1)
                act.wait_ge(s_u[i], Q_BLOCKS + h)
                nc.scalar.activation(hqT[:, i, :, 0:ROWS],
                                     PS16[:, 7, 0:512].rearrange("p (k n) -> p k n", k=4)[:, :, 0:ROWS],
                                     ACT.Copy).then_inc(s_xev[i], 1)
                silu_gate(1 - i, h + i)
                integers_x(i, h + 1)
                transposed_x(i, h + 1)

    @block.vector
    def _(dve):
        nc.vector.memset(XN[96:P, :, :], 0.0).then_inc(s_pad, 1)
        for h in range(2):
            for c in range(2):
                nc.vector.memset(sel[h * HD:(h + 1) * HD, c:c + 1], float(h == c)).then_inc(s_pad, 1)
        dve.wait_ge(s_fill, 3)
        dve.wait_ge(s_edges, 64)
        nc.vector.scalar_tensor_tensor(key[:, 0:FULL], iedge[:, 0, 0:FULL], float(A_PITCH), iedge[:, 1, 0:FULL],
                                       ALU.mult, ALU.add).then_inc(s_key, 1)
        nc.vector.scalar_tensor_tensor(key[0:TAIL, FULL:FULL + 1], iedge[0:TAIL, 0, FULL:FULL + 1], float(A_PITCH),
                                       iedge[0:TAIL, 1, FULL:FULL + 1], ALU.mult, ALU.add).then_inc(s_key, 1)
        dve.wait_ge(s_key, 2)
        nc.vector.tensor_tensor(away[:, :], away[:, :], key[:, :], ALU.subtract).then_inc(s_key, 1)
        dve.wait_ge(s_bdh, 1)
        nc.vector.tensor_tensor(bdL[:, :, :], by_block(two_banks(0)), bdH[:, :, :].bitcast(F32),
                                ALU.subtract).then_inc(s_bdl, 1)

        for g in range(GROUPS):
            dve.wait_ge(s_x[g], 32)
            if g:
                dve.wait_ge(s_st, 4 * g)
            for t in range(GT):
                for c in range(2):
                    nc.vector.bn_stats(stats[0:ROWS, t, c, :], X[0:ROWS, g * GT + t, c * 512:(c + 1) * 512]).then_inc(s_stc, 1)
            dve.wait_ge(s_stc, 8 * (g + 1))
            for t in range(GT):
                nc.vector.bn_aggr(mv[0:ROWS, g * GT + t, :], stats[0:ROWS, t, :, :].rearrange("p c n -> p (c n)")).then_inc(s_st, 1)
        dve.wait_ge(s_st, TILES)
        dve.wait_ge(s_std, 1)
        nc.vector.reciprocal(rstd[0:ROWS, :], std[0:ROWS, :]).then_inc(s_rstd, 1)
        dve.wait_ge(s_rstd, 1)
        dve.wait_ge(s_pad, 5)
        with dve.Fori(0, TILES // 2) as h:
            for i in range(2):
                t = h * 2 + i
                dve.wait_ge(s_xtr[i], h)
                nc.vector.tensor_scalar(XN[0:ROWS, i, :], X[0:ROWS, bass.ds(t, 1), :].rearrange("p o n -> p (o n)"),
                                        mv[0:ROWS, bass.ds(t, 1), 0], rstd[0:ROWS, bass.ds(t, 1)],
                                        ALU.subtract, ALU.mult).then_inc(s_xn[i], 1)
        dve.wait_ge(s_const, 8)
        dve.wait_ge(s_ew, 32)
        for b in range(AHEAD):
            dve.wait_ge(s_row[b], 32)
            for i in range(PAIRS):
                edge_pair(dve, b * PAIRS + i, b * (PAIRS // 2) + i // 2, b, i)
            edge_flags(dve, b)

        def low_of_group_tile(n_group, t, n):
            dve.wait_ge(s_xgh, n)
            cols = (bass.ds(n_group % 2, 1), slice(None), slice(t * ROWS, (t + 1) * ROWS))
            nc.vector.tensor_tensor(xgL[(slice(None),) + cols].rearrange("p o k r -> p (o k) r"), xg[:, t],
                                    xgH[(slice(None),) + cols].rearrange("p o k r -> p (o k) r").bitcast(F32),
                                    ALU.subtract).then_inc(s_xgl, 1)

        for t in range(GT):
            low_of_group_tile(0, t, t + 1)
        for mat in range(2):
            for j in range(KT):
                dve.wait_ge(s_wh[j % 2], mat * (KT // 2) + j // 2 + 1)
                cols = slice(j * P, (j + 1) * P)
                nc.vector.tensor_tensor(WL[:, :, cols], by_block(two_banks(j % 2)), WH[:, :, cols].bitcast(F32),
                                        ALU.subtract).then_inc(s_wl[j % 2], 1)
            with dve.Fori(0, GROUPS) as g:
                it = g + mat * GROUPS
                for j in range(KT):
                    m = it * (KT // 2) + j // 2
                    dve.wait_ge(s_sq[j % 2], m + 1)
                    nc.vector.scalar_tensor_tensor(qL[:, j % 2, :], PS[:, 4 + j % 2, 0:GN], bqk[:, mat, j:j + 1],
                                                   qH[:, j % 2, :].bitcast(F32), ALU.add,
                                                   ALU.subtract).then_inc(s_ql[j % 2], 1)
                    if j < GT:
                        low_of_group_tile(it + 1, j, it * GT + GT + j + 1)
                    b = it * PER_IT + AHEAD + j // 2
                    if j % 2 == 0:
                        dve.wait_ge(s_row[(j // 2) % 2], (it * (PER_IT // 2) + AHEAD // 2 + j // 4 + 1) * 32)
                    for i in range(2):
                        edge_pair(dve, b * PAIRS + (j % 2) * 2 + i, b * (PAIRS // 2) + j % 2, (j // 2) % 2, (j % 2) * 2 + i)
                    if j % 2:
                        edge_flags(dve, b)
        for i in range(2):
            dve.wait_ge(s_sq[i], ITERS * KT // 2)
        nc.vector.tensor_reduce(norms[:, 0, :], ssq[:, :].rearrange("p (m n) -> p m n", m=2), AX.X, ALU.add).then_inc(s_n[0], 1)
        dve.wait_ge(s_n[2], 1)
        nc.vector.reciprocal(norms[:, 2, :], norms[:, 1, :]).then_inc(s_n[3], 1)
        dve.wait_ge(s_n[3], 1)
        nc.vector.tensor_tensor(norms[:, 3, :], PS[:, 0, 0:2], norms[:, 2, :], ALU.mult).then_inc(s_n[4], 1)
        dve.wait_ge(s_n[4], 1)
        nc.vector.tensor_tensor(norms[:, 3, :], norms[:, 3, :], norms[:, 2, :], ALU.mult).then_inc(s_n[4], 1)
        dve.wait_ge(s_n[5], 1)
        nc.vector.tensor_scalar(norms[:, 5, :], norms[:, 4, :], HD ** -0.5, None, ALU.mult).then_inc(s_n[6], 1)
        dve.wait_ge(s_n[6], 1)
        nc.vector.tensor_tensor(norms[:, 6, 0:1], norms[:, 5, 0:1], norms[:, 5, 1:2], ALU.mult).then_inc(s_n[7], 1)
        for k in range(KT):
            dve.wait_ge(s_w2h, k + 1)
            nc.vector.tensor_tensor(WL[:, k, :], wst2[:, k % 2, :], WH[:, k, :].bitcast(F32), ALU.subtract).then_inc(s_w2l, 1)

        def low_of_tile(i, m):
            dve.wait_ge(s_xth[i], m + 1)
            nc.vector.tensor_tensor(xtL[i][:, :, :], xt[:, i], xtH[i][:, :, :].bitcast(F32), ALU.subtract).then_inc(s_xtl[i], 1)

        low_of_tile(0, 0)
        with dve.Fori(0, TILES // 2) as h:
            for i in range(2):
                low_of_tile(1 - i, h + i)
        for j in range(KT):
            dve.wait_ge(s_wh[j % 2], KT + j // 2 + 1)
            cols = slice(j * P, (j + 1) * P)
            nc.vector.tensor_tensor(WL[:, :, cols], by_block(two_banks(j % 2)), WH[:, :, cols].bitcast(F32),
                                    ALU.subtract).then_inc(s_wl[j % 2], 1)
        dve.wait_ge(s_n[7], 1)
        dve.wait_ge(s_bv, 16)
        with dve.Fori(0, TILES // 2) as h:
            for i in range(2):
                n = (h * 2 + i) * 5
                low_of_tile(1 - i, h + TILES // 2 + i)
                dve.wait_ge(s_exp[i], h * 2 + 2)
                nc.vector.scalar_tensor_tensor(ut[:, i, 0], ut[:, i, 0], norms[:, 6, 0:1], ut[:, i, 1],
                                               ALU.mult, ALU.mult).then_inc(s_phi[i], 1)
                v = two_banks(i)[0:ROWS]
                v_heads = v.rearrange("p (h n) -> p h n", h=HEADS)
                dve.wait_ge(s_mm[i], h + TILES // 2 + 1)
                nc.vector.tensor_tensor(v, v, bvb[0:ROWS, :], ALU.add).then_inc(s_vc, 1)
                dve.wait_ge(s_s[i], h + 1)
                nc.vector.tensor_copy(s_sb[0:ROWS, i, :], PS[0:ROWS, 4 + i, 0:HEADS]).then_inc(s_vc, 1)
                nc.vector.reciprocal(rs_sb[0:ROWS, i, :], PS[0:ROWS, 4 + i, 0:HEADS]).then_inc(s_vc, 1)
                dve.wait_ge(s_vc, n + 3)
                nc.vector.tensor_tensor(v_heads, v_heads, s_sb[0:ROWS, i, :, None].to_broadcast([ROWS, HEADS, HD]),
                                        ALU.mult).then_inc(s_vc, 1)
                dve.wait_ge(s_vc, n + 4)
                nc.vector.tensor_tensor(v_heads, v_heads, rs_sb[0:ROWS, i, :, None].to_broadcast([ROWS, HEADS, HD]),
                                        ALU.mult).then_inc(s_vc, 1)
                dve.wait_ge(s_vc, n + 5)
                dve.wait_ge(s_zx[i], h * 32 + 32)
                nc.vector.tensor_tensor(zx[0:ROWS, i, :], v, zx[0:ROWS, i, :], ALU.add).then_inc(s_z[i], 1)
        half = TILES // 2

        def low_of_sources(s, i, m):
            dve.wait_ge(s_hi5[i], m + 1)
            nc.vector.tensor_tensor(AL[i][0:ROWS, :], Araw[0:ROWS, i, :], AH[i][0:ROWS, :].bitcast(F32), ALU.subtract)
            nc.vector.tensor_tensor(SL[0:ROWS, i, :], S[0:ROWS, bass.ds(s, 1), :].rearrange("p o n -> p (o n)"),
                                    SH[0:ROWS, i, :].bitcast(F32), ALU.subtract).then_inc(s_lo5[i], 1)

        for i in range(2):
            low_of_sources(i, i, 0)
        with dve.Fori(0, GROUPS) as g:
            with dve.Fori(0, half - 1) as h:
                for i in range(2):
                    low_of_sources(h * 2 + 2 + i, i, g * half + h + 1)
            low_of_sources(0, 0, g * half + half)
            dve.wait_ge(s_zin, g * 32 + 32)
            for d in range(GT):
                if d < GT - 1:
                    dve.wait_ge(s_acc[d], g + 1)
                else:
                    dve.wait_ge(s_pe5[1], g * half + half)
                nc.vector.tensor_tensor(zr[0:ROWS, d, :], two_banks(d)[0:ROWS], zr[0:ROWS, d, :], ALU.add).then_inc(s_r[d], 1)
            low_of_sources(1, 1, g * half + half)
            for d in range(GT):
                dve.wait_ge(s_r[d], g + 1)
                for c in range(2):
                    nc.vector.bn_stats(stats[0:ROWS, d, c, :], zr[0:ROWS, d, c * 512:(c + 1) * 512]).then_inc(s_rst, 1)
            dve.wait_ge(s_rst, g * 8 + 8)
            dve.sem_inc(s_go2, 1)
            for d in range(GT):
                nc.vector.bn_aggr(group_mv[0:ROWS, d, :], stats[0:ROWS, d, :, :].rearrange("p c n -> p (c n)")).then_inc(s_rag, 1)
            dve.wait_ge(s_rag, g * GT + GT)
            nc.vector.tensor_copy(mv[0:ROWS, bass.ds(g * GT, GT), :], group_mv[0:ROWS, :, :]).then_inc(s_rmv, 1)
            dve.wait_ge(s_rmv, g + 1)
        dve.wait_ge(s_std, 1 + 1)
        nc.vector.reciprocal(rstd[0:ROWS, :], std[0:ROWS, :]).then_inc(s_rstd, 1)
        for f in range(3):
            dve.wait_ge(s_fabs, 4 * (f + 1))
            nc.vector.tensor_reduce(wsum[:, f:f + 1], wabs[:, 4 * f:4 * f + 4], AX.X, ALU.add).then_inc(s_fs, 1)
        for f in range(3):
            dve.wait_ge(s_ftot, f + 1)
            nc.vector.tensor_scalar(wq_sc[:, f, 0:1], PS[:, 4 + f, 0:1], 1.0 / (INNER * D), QUANT_EPS,
                                    ALU.mult, ALU.max).then_inc(s_fc, 1)
            dve.wait_ge(s_fc, 6 * f + 1)
            nc.vector.reciprocal(wq_sc[:, f, 1:2], wq_sc[:, f, 0:1]).then_inc(s_fc, 1)
            dve.wait_ge(s_fc, 6 * f + 2)
            nc.vector.reciprocal(wq_sc[:, f, 2:3], wq_sc[:, f, 1:2]).then_inc(s_fc, 1)
            w = fw[f][:, :, :]
            nc.vector.tensor_scalar(w, w, wq_sc[:, f, 1:2], 1.0, ALU.mult, ALU.min).then_inc(s_fc, 1)
            dve.wait_ge(s_fc, 6 * f + 4)
            nc.vector.tensor_scalar(w, w, -1.0, ROUND, ALU.max, ALU.add).then_inc(s_fc, 1)
            dve.wait_ge(s_fc, 6 * f + 5)
            nc.vector.tensor_scalar(fq[f][:, :, :], w, ROUND, None, ALU.subtract).then_inc(s_fc, 1)

        dve.wait_ge(s_rstd, 1 + 1)
        dve.wait_ge(s_fc, 18)

        def front(t, i, m, n):
            sc = x_sc[0:ROWS, i, :]
            c = rc[0:ROWS, i, :]
            dve.wait_ge(s_zx[i], ZX_END + m * 32 + 32)
            dve.wait_ge(s_rq16[i], m)
            nc.vector.tensor_scalar(c, rt[0:ROWS, i, :], mv[0:ROWS, bass.ds(t, 1), 0], rstd[0:ROWS, bass.ds(t, 1)],
                                    ALU.subtract, ALU.mult).then_inc(s_f6, 1)
            dve.wait_ge(s_f6, n + 1)
            nc.vector.tensor_reduce(sc[:, 0:1], c, AX.X, ALU.max, apply_absolute_value=True).then_inc(s_f6, 1)
            dve.wait_ge(s_f6, n + 2)
            nc.vector.tensor_scalar(sc[:, 0:1], sc[:, 0:1], QUANT_EPS, 1.0 / 127.0, ALU.max, ALU.mult).then_inc(s_f6, 1)
            dve.wait_ge(s_f6, n + 3)
            nc.vector.reciprocal(sc[:, 1:2], sc[:, 0:1]).then_inc(s_f6, 1)
            dve.wait_ge(s_h[i], m)
            nc.vector.tensor_tensor(sc[:, 2:3], sc[:, 0:1], wq_sc[0:ROWS, 0, 2:3], ALU.mult).then_inc(s_f6, 1)
            nc.vector.tensor_tensor(sc[:, 3:4], sc[:, 0:1], wq_sc[0:ROWS, 1, 2:3], ALU.mult).then_inc(s_f6, 1)
            dve.wait_ge(s_f6, n + 6)
            nc.vector.tensor_scalar(c, c, sc[:, 1:2], 127.0, ALU.mult, ALU.min).then_inc(s_f6, 1)
            dve.wait_ge(s_f6, n + 7)
            nc.vector.tensor_scalar(c, c, -128.0, ROUND, ALU.max, ALU.add).then_inc(s_rq[i], 1)

        for i in range(2):
            front(i, i, 0, 7 * i)
        with dve.Fori(0, half) as h:
            for i in range(2):
                t = h * 2 + i
                sc, hh = h_sc[0:ROWS, i, :], hid[0:ROWS, i, :]
                n = t * 5
                dve.wait_ge(s_gate[i], h + 1)
                dve.wait_ge(s_hq16[i], h)
                nc.vector.scalar_tensor_tensor(hh, PS[0:ROWS, 2 * i + 1, :], x_sc[0:ROWS, i, 3:4], gate[0:ROWS, i, :],
                                               ALU.mult, ALU.mult).then_inc(s_h[i], 1)
                dve.wait_ge(s_h[i], h + 1)
                nc.vector.tensor_reduce(sc[:, 0:1], hh, AX.X, ALU.max, apply_absolute_value=True).then_inc(s_h6, 1)
                dve.wait_ge(s_h6, n + 1)
                nc.vector.tensor_scalar(sc[:, 0:1], sc[:, 0:1], QUANT_EPS, 1.0 / 127.0, ALU.max, ALU.mult).then_inc(s_h6, 1)
                dve.wait_ge(s_h6, n + 2)
                nc.vector.reciprocal(sc[:, 1:2], sc[:, 0:1]).then_inc(s_h6, 1)
                nc.vector.tensor_tensor(sc[:, 2:3], sc[:, 0:1], wq_sc[0:ROWS, 2, 2:3], ALU.mult).then_inc(s_h6, 1)
                dve.wait_ge(s_h6, n + 4)
                nc.vector.tensor_scalar(hh, hh, sc[:, 1:2], 127.0, ALU.mult, ALU.min).then_inc(s_h6, 1)
                dve.wait_ge(s_h6, n + 5)
                nc.vector.tensor_scalar(hh, hh, -128.0, ROUND, ALU.max, ALU.add).then_inc(s_hq[i], 1)
                dve.wait_ge(s_u[i], Q_BLOCKS + h + 1)
                dve.wait_ge(s_uout[i], Q_BLOCKS * 16 + h * 32)
                nc.vector.scalar_tensor_tensor(fin[0:ROWS, i, :], PS[0:ROWS, 4:6, :].rearrange("p b n -> p (b n)"),
                                               sc[:, 2:3], rt[0:ROWS, i, :], ALU.mult, ALU.add).then_inc(s_z[i], 1)
                front((t + 2) % TILES, i, h + 1, (t + 2) * 7)

    @block.tensor
    def _(pe):
        def transposes(slot, rows):
            for k in range(KT):
                last = nc.tensor.transpose(by_block(two_banks(slot))[:, k, :], rows[:, k * P:(k + 1) * P], ident[:, :])
            return last

        pe.wait_ge(s_const, 8)
        pe.wait_ge(s_bd, 32)
        transposes(0, wst[:, 0, :]).then_inc(s_bdtr, 1)
        pe.wait_ge(s_key, 2)
        pe.wait_ge(s_ew, 32)
        for q, t in enumerate((key, ew)):
            for b in range(4):
                last = nc.tensor.transpose(PS[0:CT, 4 + q, b * P:(b + 1) * P], t[:, b * CT:(b + 1) * CT], ident[:, :])
            last.then_inc(s_ktr, 1)
        pe.wait_ge(s_bdl, 1)
        with pe.Fori(0, TILES // 2) as h:
            for i in range(2):
                pe.wait_ge(s_xn[i], h + 1)
                pe.wait_ge(s_xev[i], h)
                transposes(i, XN[:, i, :]).then_inc(s_xtr[i], 1)
        for i in range(2):
            pe.wait_ge(s_xev[i], TILES // 2)
        pe.wait_ge(s_ksb, 2)
        for mat in range(2):
            for j in range(KT):
                m = mat * (KT // 2) + j // 2
                pe.wait_ge(s_wst[j % 2], m * 16 + 16)
                pe.wait_ge(s_wh[j % 2], m)
                pe.wait_ge(s_wl[j % 2], m)
                transposes(j % 2, wst[:, j % 2, :]).then_inc(s_wtr[j % 2], 1)
            for i in range(2):
                pe.wait_ge(s_wl[i], (mat + 1) * KT // 2)
            with pe.Fori(0, GROUPS) as g:
                it = g + mat * GROUPS
                pe.wait_ge(s_xgl, it * GT + GT)

                def maps(j):
                    m = it * (KT // 2) + j // 2
                    pe.wait_ge(s_ql[j % 2], m + 1)
                    pe.wait_ge(s_uev[j % 2], m)
                    product3(PS[:, 6 + j % 2, 0:GN], bdH[:, j, :], bdL[:, j, :], qH[:, j % 2, :], qL[:, j % 2, :],
                             True, True).then_inc(s_u[j % 2], 1)

                for j in range(KT):
                    m = it * (KT // 2) + j // 2
                    pe.wait_ge(s_sq[j % 2], m)
                    pe.wait_ge(s_ql[j % 2], m)
                    cols = slice(j * P, (j + 1) * P)
                    for k in range(KT):
                        rh, rl = (b[:, bass.ds(it % 2, 1), k, :].rearrange("p o n -> p (o n)") for b in (xgH, xgL))
                        last = product3(PS[:, 4 + j % 2, 0:GN], WH[:, k, cols], WL[:, k, cols], rh, rl,
                                        k == 0, k == KT - 1)
                    last.then_inc(s_q[j % 2], 1)
                    if j:
                        maps(j - 1)
                maps(KT - 1)
        pe.wait_ge(s_n[0], 1)
        nc.tensor.matmul(PS[:, 0, 0:2], ones[:, :], norms[:, 0, :], start=True, stop=True).then_inc(s_n[1], 1)
        pe.wait_ge(s_n[4], 2)

        def tile_products(i):
            for k in range(KT):
                for c in range(2):
                    cols = slice(c * 512, (c + 1) * 512)
                    last = product3(PS[0:ROWS, 2 * i + c, :], xtH[i][:, k, :], xtL[i][:, k, :], WH[:, k, cols],
                                    WL[:, k, cols], k == 0, k == KT - 1)
            last.then_inc(s_mm[i], 1)

        pe.wait_ge(s_pad, 5)
        pe.wait_ge(s_w2l, KT)
        with pe.Fori(0, TILES // 2) as h:
            for i in range(2):
                pe.wait_ge(s_xtl[i], h + 1)
                pe.wait_ge(s_supev[i], h)
                tile_products(i)
        for j in range(KT):
            pe.wait_ge(s_wst[j % 2], (KT + KT // 2 + j // 2) * 16 + 16)
            pe.wait_ge(s_supev[j % 2], TILES // 2)
            pe.wait_ge(s_wl[j % 2], KT + j // 2)
            transposes(j % 2, wst2[:, j % 2, :]).then_inc(s_wtr[j % 2], 1)
        for i in range(2):
            pe.wait_ge(s_wl[i], KT + KT // 2)
        with pe.Fori(0, TILES // 2) as h:
            for i in range(2):
                pe.wait_ge(s_xtl[i], h + TILES // 2 + 1)
                pe.wait_ge(s_z[i], h)
                tile_products(i)
                pe.wait_ge(s_phi[i], h + 1)
                for j in range(KT):
                    last = nc.tensor.matmul(PS[0:ROWS, 4 + i, 2 * j:2 * j + 2], ut[:, i, 0, j, :], sel[:, :],
                                            start=True, stop=True)
                last.then_inc(s_s[i], 1)
        half = TILES // 2
        for i in range(2):
            pe.wait_ge(s_z[i], half)

        def sources(g, i, m, first, last_one):
            pe.wait_ge(s_lo5[i], m + 1)
            for d in range(GT):
                if first:
                    pe.wait_ge(s_r[d], g)
                rows = slice(d * ROWS, (d + 1) * ROWS)
                for c in range(2):
                    cols = slice(c * 512, (c + 1) * 512)
                    last = product3(PS[0:ROWS, 2 * d + c, :], AH[i][0:ROWS, rows], AL[i][0:ROWS, rows],
                                    SH[0:ROWS, i, cols], SL[0:ROWS, i, cols], first, last_one)
                if last_one and d < GT - 1:
                    last.then_inc(s_acc[d], 1)
            last.then_inc(s_pe5[i], 1)

        with pe.Fori(0, GROUPS) as g:
            for i in range(2):
                sources(g, i, g * half, i == 0, False)
            with pe.Fori(1, half - 1) as h:
                for i in range(2):
                    sources(g, i, g * half + h, False, False)
            for i in range(2):
                sources(g, i, g * half + half - 1, False, i == 1)
        for d in range(GT):
            pe.wait_ge(s_r[d], GROUPS)
        for f in range(3):
            pe.wait_ge(s_fs, f + 1)
            nc.tensor.matmul(PS[:, 4 + f, 0:1], ones[:, :], wsum[:, f:f + 1], start=True, stop=True).then_inc(s_ftot, 1)
        pe.wait_ge(s_id16, 1)
        for f, (wT, n) in enumerate(((wgT, KT), (wuT, KT), (wdT, 4))):
            pe.wait_ge(s_fc, 6 * f + 6)
            outs = 32 // n
            flat = fq[f][:, :, :].rearrange("p a n -> p (a n)")
            for c in range(4):
                pe.wait_ge(s_fT[c % 2], 2 * f + c // 2)
                for e in range(8):
                    k, o = divmod(8 * c + e, outs)
                    last = nc.tensor.transpose(PS16[:, c % 2, e * P:(e + 1) * P], flat[:, (o * n + k) * P:(o * n + k + 1) * P],
                                               ident16[:, :])
                last.then_inc(s_ftr[c % 2], 1)
        for i in range(2):
            pe.wait_ge(s_fT[i], 6)

        def transpose_x(i, m):
            pe.wait_ge(s_rq16[i], m + 1)
            if i == 0:
                pe.wait_ge(s_rqT[1], m)
            else:
                pe.wait_ge(s_rqT[0], m + 1)
            for k in range(KT):
                last = nc.tensor.transpose(PS16[:, 6, k * P:k * P + ROWS], rq16[0:ROWS, i, k * P:(k + 1) * P],
                                           ident16[0:ROWS, 0:ROWS])
            last.then_inc(s_rtr[i], 1)

        def gate_up(i, m):
            pe.wait_ge(s_rqT[i], m + 1)
            pe.wait_ge(s_h[i], m)
            for c, wT in enumerate((wgT, wuT)):
                for k in range(KT):
                    last = nc.tensor.matmul(PS[0:ROWS, 2 * i + c, :], rqT[:, i, k, 0:ROWS], wT[:, k, :],
                                            start=k == 0, stop=k == KT - 1)
            last.then_inc(s_q[i], 1)

        transpose_x(0, 0)
        gate_up(0, 0)
        transpose_x(1, 0)
        with pe.Fori(0, half) as h:
            for i in range(2):
                gate_up(1 - i, h + i)
                pe.wait_ge(s_hq16[i], h + 1)
                if i == 0:
                    pe.wait_ge(s_xev[1], HALF + h)
                else:
                    pe.wait_ge(s_xev[0], HALF + h + 1)
                for k in range(INNER // P):
                    last = nc.tensor.transpose(PS16[:, 7, k * P:k * P + ROWS], hq16[0:ROWS, i, k * P:(k + 1) * P],
                                               ident16[0:ROWS, 0:ROWS])
                last.then_inc(s_xtr[i], 1)
                pe.wait_ge(s_xev[i], HALF + h + 1)
                if i == 0:
                    pe.wait_ge(s_z[1], HALF + h)
                else:
                    pe.wait_ge(s_z[0], HALF + h + 1)
                for c in range(2):
                    for k in range(INNER // P):
                        last = nc.tensor.matmul(PS[0:ROWS, 4 + c, :], hqT[:, i, k, 0:ROWS],
                                                wdT[:, k, c * 512:(c + 1) * 512], start=k == 0, stop=k == INNER // P - 1)
                last.then_inc(s_u[i], 1)
                transpose_x(i, h + 1)

    block_cm.__exit__(None, None, None)


_INS = ['x', 'src', 'dst', 'edge_weight', 'L0_gnn_W', 'L0_mix_Wq', 'L0_mix_bq', 'L0_mix_Wk', 'L0_mix_bk',
        'L0_mix_Wv', 'L0_mix_bv', 'L0_mix_weights', 'L0_ffn_w_gate', 'L0_ffn_w_up', 'L0_ffn_w_down']


def kernel(**inputs):
    import concourse.bacc as bacc
    from concourse.bass_utils import run_bass_kernel_spmd

    nc = bacc.Bacc("TRN2", target_bir_lowering=False, num_devices=1)
    arrays, args = {}, []
    for name in _INS:
        a = np.ascontiguousarray(inputs[name])
        arrays["in_" + name] = a
        args.append(nc.dram_tensor("in_" + name, a.shape, mybir.dt.from_np(a.dtype), kind="ExternalInput").ap())
    args.append(nc.dram_tensor("out_r", (NODES, D), F32, kind="ExternalOutput").ap())
    layer_kernel(nc, *args)
    r = run_bass_kernel_spmd(nc, [arrays], core_ids=[0])
    return r.results[0]["out_r"]
```

```python
import numpy as np

import concourse.bass as bass
from concourse import mybir

F32 = mybir.dt.float32
F32R = mybir.dt.float32r
BF16 = mybir.dt.bfloat16
I32 = mybir.dt.int32
U32 = mybir.dt.uint32
ALU = mybir.AluOpType
ACT = mybir.ActivationFunctionType
AX = mybir.AxisListType

P = 128
NODES = 2500
EDGES = 42500
D = 1024
KT = D // P
INNER = 512
HEADS = 16
HD = D // HEADS
ROWS = 125
TILES = NODES // ROWS
GT = 4
GN = GT * ROWS
GROUPS = TILES // GT
LN_EPS = 1e-5
QUANT_EPS = 1e-5
ROUND = 1.5 * 2.0 ** 23

A_PITCH = 2560
CH_BLOCK = 8
PAIRS = CH_BLOCK // 2
FULL = EDGES // P
TAIL = EDGES - FULL * P
AHEAD = 2
PER_IT = 4
ITERS = 2 * GROUPS
BLOCKS = AHEAD + PER_IT * ITERS
CHUNKS = BLOCKS * CH_BLOCK
ROWS_C = CHUNKS
assert CHUNKS * P >= EDGES
CT = ROWS_C // 4

SBUF_AT = 16640
SMALL_AT = SBUF_AT
KEYS_AT = SMALL_AT + 4096
W_AT = KEYS_AT + 5 * 4 * ROWS_C
S_AT = W_AT + 2 * 4 * KT * D
E_AT = S_AT + 4 * TILES * D
END_AT = 229368


def split_rows(eng, dst, src, sem):
    cut = 112
    eng.dma_start(dst[0:cut], src[0:cut]).then_inc(sem, 16)
    eng.dma_start(dst[cut:ROWS], src[cut:ROWS]).then_inc(sem, 16)


def layer_kernel(nc, x, src, dst, edge_weight, W, Wq, bq, Wk, bk, Wv, bv, mix_w, w_gate, w_up, w_down, out):
    A = nc.dram_tensor("A_dense", (A_PITCH, A_PITCH), F32).ap()
    key_d = nc.dram_tensor("key_rows", (ROWS_C, P), F32).ap()
    ew_d = nc.dram_tensor("weight_rows", (ROWS_C, P), F32).ap()
    xnT_d = nc.dram_tensor("xnT", (TILES, P, KT, ROWS), F32).ap()
    uT_d = nc.dram_tensor("uT", (2, P, KT, NODES), F32).ap()
    z_d = nc.dram_tensor("z", (NODES, D), F32).ap()
    r_d = nc.dram_tensor("r", (NODES, D), F32).ap()
    wT_d = nc.dram_tensor("ternary", (12, P, D), BF16).ap()

    cursor = {}

    def zone(label, at, end):
        cursor[label] = at

        def put(name, shape, dt=F32):
            size = 2 if dt == BF16 else 4
            here = cursor[label]
            cursor[label] = here + (int(np.prod(shape[1:])) * size + 31) // 32 * 32
            assert cursor[label] <= end, (name, cursor[label], end)
            return nc.alloc_sbuf_tensor_at(name, shape, dt, offset=here)
        return put

    small = zone("small", SMALL_AT, KEYS_AT)
    ident = small("ident", [P, P])
    ident16 = small("ident16", [P, P], BF16)
    earlier = small("earlier", [P, 2, P])
    sel = small("sel", [P, 2])
    eps = small("eps", [P, 1])
    neg_round = small("neg_round", [P, 1])
    bqk = small("bqk", [P, 2, KT])
    mv = small("mv", [P, TILES, 2])
    std = small("std", [P, TILES])
    rstd = small("rstd", [P, TILES])
    stats = small("stats", [P, GT, 2, 6])
    group_mv = small("group_mv", [P, GT, 2])
    ssq = small("ssq", [P, 2 * GROUPS * KT])
    norms = small("norms", [P, 8, 2])
    w_slot = small("w_slot", [P, 2, CH_BLOCK])
    to_dummy = small("to_dummy", [P, 2, CH_BLOCK])
    cell_slot = small("cell_slot", [P, 2, CH_BLOCK], U32)
    wabs = small("wabs", [P, 12])
    wsum = small("wsum", [P, 3])
    wq_sc = small("wq_sc", [P, 3, 4])
    f_sc = small("f_sc", [P, GT])
    x_back = small("x_back", [P, TILES])
    g_back = small("g_back", [P, TILES])
    u_back = small("u_back", [P, TILES])
    h_sc = small("h_sc", [P, 2, 4])

    keys = zone("keys", KEYS_AT, W_AT)
    key = keys("key", [P, ROWS_C])
    ew = keys("ew", [P, ROWS_C])
    away = keys("away", [P, ROWS_C])
    wtot = keys("wtot", [P, ROWS_C])
    dup = keys("dup", [P, ROWS_C])

    late_keys = zone("late_keys", KEYS_AT + 4 * ROWS_C, W_AT)
    s_all = late_keys("s_all", [P, TILES, HEADS])
    assert cursor["late_keys"] <= KEYS_AT + 2 * 4 * ROWS_C

    wz = zone("W", W_AT, S_AT)
    WH = wz("WH", [P, KT, D], F32R)
    WL = wz("WL", [P, KT, D], F32R)
    w1 = zone("W1", W_AT, S_AT)
    XT = w1("XT", [P, GT, KT, ROWS])
    iedge = w1("iedge", [P, 2, ROWS_C], I32)
    kT_sb = w1("kT_sb", [P, 8, P])

    X = zone("S1", S_AT, E_AT)("X", [P, TILES, D])
    s2 = zone("S2", S_AT, E_AT)
    xg = s2("xg", [P, GT, KT, ROWS])
    xgH = s2("xgH", [P, 2, KT, GN], F32R)
    xgL = s2("xgL", [P, 2, KT, GN], F32R)
    S = zone("S3", S_AT, E_AT)("S", [P, TILES, D])

    e1 = zone("E1", E_AT, END_AT)
    wst = e1("wst", [P, 2, D])
    keyrow = e1("keyrow", [P, 2, CH_BLOCK * P])
    ewrow = e1("ewrow", [P, 2, CH_BLOCK * P])
    junk = e1("junk", [P, 2, 7, P], BF16)
    bdH = e1("bdH", [P, KT, P], F32R)
    bdL = e1("bdL", [P, KT, P], F32R)
    at = cursor["E1"]
    XN = zone("E1a", at, END_AT)("XN", [P, 2, D])
    e1b = zone("E1b", at, END_AT)
    qH = e1b("qH", [P, 2, GN], F32R)
    qL = e1b("qL", [P, 2, GN], F32R)
    usb = e1b("usb", [P, 2, GN])
    zeros = e1b("zeros", [P, A_PITCH // 4])
    squares = e1b("squares", [P, 2, GN], BF16)

    zx = zone("E2x", E_AT, END_AT)("zx", [P, 2, D])
    e2 = zone("E2", cursor["E2x"], END_AT)
    xt = e2("xt", [P, 2, KT, ROWS])
    xtH = [e2(f"xtH{i}", [P, KT, ROWS], F32R) for i in range(2)]
    xtL = [e2(f"xtL{i}", [P, KT, ROWS], F32R) for i in range(2)]
    bvb = e2("bvb", [P, D])
    rows2 = zone("E2r", cursor["E2"] - 4 * D, END_AT)("rows2", [P, D])
    at = cursor["E2"]
    e2a = zone("E2a", at, END_AT)
    uu = e2a("uu", [P, 2, 2, 2, GN])
    rows3 = zone("E2s", cursor["E2a"] - 4 * 4 * GN, END_AT)("rows3", [P, 2, D])
    e2b = zone("E2b", at, END_AT)
    rs_all = e2b("rs_all", [P, TILES, HEADS])
    fwb = e2b("fwb", [P, 2, D])
    fqb = e2b("fqb", [P, 2, D], BF16)
    fTb = e2b("fTb", [P, 2, D], BF16)

    w3 = zone("W3", W_AT, S_AT)
    wT = w3("wT", [P, 3, 4, D], BF16)
    SH = w3("SH", [P, 2, D], F32R)
    SL = w3("SL", [P, 2, D], F32R)
    zr = w3("zr", [P, GT, D])
    rc = w3("rc", [P, 2, D])
    e3 = zone("E3", E_AT, END_AT)
    rq16 = e3("rq16", [P, TILES, D], BF16)
    Araw = e3("Araw", [P, 2, GN])
    AH = [e3(f"AH{i}", [P, GN], F32R) for i in range(2)]
    AL = [e3(f"AL{i}", [P, GN], F32R) for i in range(2)]

    s6 = zone("S6", S_AT, E_AT)
    rt = s6("rt", [P, 2, D])
    rqT = s6("rqT", [P, 2, KT, P], BF16)
    gate = s6("gate", [P, 2, INNER])
    hid = s6("hid", [P, 2, INNER])
    hq16 = s6("hq16", [P, 2, INNER], BF16)
    hqT = s6("hqT", [P, 2, INNER // P, P], BF16)
    fin = s6("fin", [P, 2, D])

    PS = nc.alloc_psum_tensor("PS", [P, 8, 512], F32)
    PS16 = PS[:, :, :].bitcast(BF16)

    def two_banks(slot):
        return PS[:, 2 * slot:2 * slot + 2, :].rearrange("p b n -> p (b n)")

    def by_block(ap):
        return ap.rearrange("p (k n) -> p k n", k=KT)

    def sem(name):
        return nc.alloc_semaphore(name)

    def sems(name, n=2):
        return [sem(f"{name}{i}") for i in range(n)]

    HALF = TILES // 2
    Q_BLOCKS = ITERS * KT // 2
    ZX_END = 32 * (HALF + 1)
    s_Ar = sems("s_Ar", 2)
    s_Azero = sems("s_Azero", 2)
    s_acc = sems("s_acc", GT)
    s_bd = sem("s_bd")
    s_ev0 = sem("s_ev0")
    s_tr0 = sem("s_tr0")
    s_bias = sem("s_bias")
    s_bv = sem("s_bv")
    s_c5 = sem("s_c5")
    s_const = sem("s_const")
    s_edges = sem("s_edges")
    s_ew = sem("s_ew")
    s_exp = sems("s_exp", 2)
    s_f6 = sem("s_f6")
    s_fT = sems("s_fT", 2)
    s_fabs = sem("s_fabs")
    s_fb = sem("s_fb")
    s_fc = sem("s_fc")
    s_fill = sem("s_fill")
    s_flags = sem("s_flags")
    s_fm = sem("s_fm")
    s_fout = sems("s_fout", 2)
    s_fq16 = sems("s_fq16", 2)
    s_fr = sems("s_fr", 2)
    s_fs = sem("s_fs")
    s_ftot = sem("s_ftot")
    s_ftr = sems("s_ftr", 2)
    s_fw = sems("s_fw", 2)
    s_gate = sems("s_gate", 2)
    s_go = sem("s_go")
    s_go2 = sem("s_go2")
    s_h = sems("s_h", 2)
    s_h6 = sem("s_h6")
    s_hi5 = sems("s_hi5", 2)
    s_hq = sems("s_hq", 2)
    s_hq16 = sems("s_hq16", 2)
    s_key = sem("s_key")
    s_kout = sem("s_kout")
    s_lo5 = sems("s_lo5", 2)
    s_mm = sems("s_mm", 2)
    s_norm = sem("s_norm")
    s_pad = sem("s_pad")
    s_pair = sems("s_pair", 2)
    s_pe5 = sems("s_pe5", 2)
    s_phi = sems("s_phi", 2)
    s_q = sems("s_q", 2)
    s_ql = sems("s_ql", 2)
    s_r = sems("s_r", GT)
    s_rmv = sem("s_rmv")
    s_rout = sem("s_rout")
    s_row = sems("s_row", 2)
    s_rq = sems("s_rq", 2)
    s_rq16 = sems("s_rq16", 2)
    s_rqT = sems("s_rqT", 2)
    s_rs = sem("s_rs")
    s_rst = sem("s_rst")
    s_rstd = sem("s_rstd")
    s_rtr = sems("s_rtr", 2)
    s_s = sems("s_s", 2)
    s_sc = sems("s_sc", 2)
    s_scp = sems("s_scp", 2)
    s_slot = sem("s_slot")
    s_sq = sems("s_sq", 2)
    s_st = sem("s_st")
    s_stc = sem("s_stc")
    s_std = sem("s_std")
    s_supev = sems("s_supev", 2)
    s_u = sems("s_u", 2)
    s_uev = sems("s_uev", 2)
    s_uout = sems("s_uout", 2)
    s_ut = sems("s_ut", 2)
    s_vc = sem("s_vc")
    s_w2h = sem("s_w2h")
    s_w2l = sem("s_w2l")
    s_wT = sem("s_wT")
    s_wh = sems("s_wh", 2)
    s_wl = sems("s_wl", 2)
    s_wst = sems("s_wst", 2)
    s_wtr = sems("s_wtr", 2)
    s_x = sems("s_x", GROUPS)
    s_xev = sems("s_xev", 2)
    s_xg = sem("s_xg")
    s_xgh = sem("s_xgh")
    s_xgl = sem("s_xgl")
    s_xn = sems("s_xn", 2)
    s_xout = sems("s_xout", 2)
    s_xTout = sems("s_xTout", GT)
    s_xt = sems("s_xt", 2)
    s_xth = sems("s_xth", 2)
    s_xtl = sems("s_xtl", 2)
    s_xtr = sems("s_xtr", 2)
    s_z = sems("s_z", 2)
    s_zin = sem("s_zin")
    s_zx = sems("s_zx", 2)

    ORDER = (0, 2, 3, 1)

    def product3(o, lh, ll, rh, rl, start, stop):
        nc.tensor.matmul(o, lh, rl, start=start, stop=False)
        nc.tensor.matmul(o, ll, rh, start=False, stop=False)
        return nc.tensor.matmul(o, lh, rh, start=False, stop=stop)

    def edge_pair(dve, pair, uses, block_slot, i):
        slot = i % 2
        row, wrow = (b[:, block_slot, 2 * i * P:(2 * i + 2) * P] for b in (keyrow, ewrow))
        dve.wait_ge(s_pair[slot], uses)
        for c in range(2):
            col = bass.ds(pair * 2 + c, 1)
            nc.vector.scalar_tensor_tensor(junk[:, slot, 2 * c:2 * c + 2, :].rearrange("p a n -> p (a n)"), row,
                                           key[:, col], wrow, ALU.is_equal, ALU.mult, accum_out=wtot[:, col])
        nc.vector.scalar_tensor_tensor(junk[:, slot, 4, :], row[:, 0:P], key[:, bass.ds(pair * 2, 1)],
                                       earlier[:, 1, :], ALU.is_equal, ALU.mult,
                                       accum_out=dup[:, bass.ds(pair * 2, 1)])
        nc.vector.scalar_tensor_tensor(junk[:, slot, 5:7, :].rearrange("p a n -> p (a n)"), row,
                                       key[:, bass.ds(pair * 2 + 1, 1)],
                                       earlier[:, :, :].rearrange("p a n -> p (a n)"), ALU.is_equal, ALU.mult,
                                       accum_out=dup[:, bass.ds(pair * 2 + 1, 1)]).then_inc(s_pair[slot], 1)

    def edge_flags(dve, b):
        for k in range(2):
            dve.wait_ge(s_pair[k], (b + 1) * (PAIRS // 2))
        cols = bass.ds(b * CH_BLOCK, CH_BLOCK)
        nc.vector.tensor_scalar(dup[:, cols], dup[:, cols], 1.0, None, ALU.min).then_inc(s_flags, 1)

    def wait_stage4(eng):
        for i in range(2):
            eng.wait_ge(s_zx[i], 32 * (HALF + 1))
            eng.wait_ge(s_xt[i], 16 * (TILES + 1))
            eng.wait_ge(s_xth[i], TILES + 1 - i)
            eng.wait_ge(s_xtl[i], TILES + 1 - i)
            eng.wait_ge(s_mm[i], TILES)
            eng.wait_ge(s_xout[i], 32 * HALF)
            eng.wait_ge(s_fout[i], 16 * 6)

    row_slots = [(wst[:, 0, :], s_wst[0]), (wst[:, 1, :], s_wst[1]), (rows2[:, :], s_x[0]),
                 (rows3[:, 0, :], s_x[1]), (rows3[:, 1, :], s_x[2])]
    counts = [16 * KT, 16 * KT, 32, 32, 32]
    row_blocks = []
    for slot in (0, 1, 2, 3, 4, 0, 1, 2) + (0, 1, 2, 3, 4, 0, 1, 3):
        counts[slot] += 16
        row_blocks.append(row_slots[slot] + (counts[slot],))

    def load_key_rows(eng, b, slot):
        for buf, dram in ((keyrow, key_d), (ewrow, ew_d)):
            eng.dma_start(buf[:, slot, :], dram[bass.ds(b * CH_BLOCK, CH_BLOCK), :].rearrange("(o c) p -> o (c p)", o=1)
                         .to_broadcast([P, CH_BLOCK * P])).then_inc(s_row[slot], 16)

    def load_row_block(eng, w, j):
        eng.dma_start(wst[:, j % 2, :], w[j * P:(j + 1) * P, :]).then_inc(s_wst[j % 2], 16)

    block_cm = nc.Block()
    block = block_cm.__enter__()

    @block.sync
    def _(sp):
        for i, v in enumerate((src, dst)):
            sp.dma_start(iedge[:, i, 0:FULL], v[0:FULL * P].rearrange("(p c) -> p c", p=P)).then_inc(s_edges, 16)
            sp.dma_start(iedge[0:TAIL, i, FULL:FULL + 1],
                         v[FULL * P:EDGES].rearrange("(p c) -> p c", c=1)).then_inc(s_edges, 16)
        sp.wait_ge(s_fill, 4)
        sp.dma_start(ew[:, 0:FULL], edge_weight[0:FULL * P].rearrange("(p c) -> p c", p=P)).then_inc(s_ew, 16)
        sp.dma_start(ew[0:TAIL, FULL:FULL + 1],
                     edge_weight[FULL * P:EDGES].rearrange("(p c) -> p c", c=1)).then_inc(s_ew, 16)
        sp.wait_ge(s_fill, 1)
        mw = mix_w.rearrange("(j h) m d -> h m j d", h=2)
        for h in range(2):
            sp.dma_start(by_block(wst[:, 0, :])[h * HD:(h + 1) * HD, :, h * HD:(h + 1) * HD], mw[h]).then_inc(s_bd, 16)
        for g in range(GROUPS):
            split_rows(sp, X[:, g * GT:(g + 1) * GT, :],
                       x[g * GN:(g + 1) * GN, :].rearrange("(t r) d -> r t d", r=ROWS), s_x[g])
        with nc.allow_non_contiguous_dma(reason="two vectors of biases"):
            for i, v in enumerate((bq, bk)):
                sp.dma_start(bqk[:, i, :], v.rearrange("(j p) -> p j", p=P)).then_inc(s_bias, 16)
        sp.wait_ge(s_tr0, 1)
        for j in range(2):
            load_row_block(sp, Wq, j)
        def load_group(g):
            sp.dma_start(xg[:, :, :, :].rearrange("p t k r -> p t (k r)"),
                         xnT_d[bass.ds(g * GT, GT)].rearrange("t p k r -> p t (k r)")).then_inc(s_xg, 16)

        for t in range(TILES):
            sp.wait_ge(s_xev[t % 2], t // 2 + 1)
            sp.dma_start(xnT_d[t].rearrange("p k r -> p (k r)"), XT[:, t % GT].rearrange("p k r -> p (k r)")).then_inc(s_xTout[t % GT], 16)
            if t == GT - 1:
                sp.wait_ge(s_kout, 32)
                for b in range(AHEAD):
                    load_key_rows(sp, b, b)
            if t == 2 * GT - 1:
                for i in range(GT):
                    sp.wait_ge(s_xTout[i], 16)
                load_group(0)
        for i in range(GT):
            sp.wait_ge(s_xTout[i], 16 * GROUPS)
        for hl in (s_xgh, s_xgl):
            sp.wait_ge(hl, GT)
        load_group(1)
        for b in range(AHEAD):
            for k in range(2):
                sp.wait_ge(s_pair[k], (b + 1) * (PAIRS // 2))
            load_key_rows(sp, b + AHEAD, b)

        def stage2_group(mat, g, last=False):
            it = g + mat * GROUPS
            for j in range(KT):
                if j:
                    out_u(mat, it, g, j - 1)
                elif isinstance(g, int) and g == 0:
                    if mat:
                        out_u(mat - 1, it - 1, GROUPS - 1, KT - 1)
                else:
                    out_u(mat, it - 1, g - 1, KT - 1)
                if last and j == 7:
                    for k in range(2):
                        sp.wait_ge(s_pair[k], (BLOCKS - 1) * PAIRS // 2)
                    load_tile(0, 0)
                if j == 4 and not last:
                    for hl in (s_xgh, s_xgl):
                        sp.wait_ge(hl, it * GT + 2 * GT)
                    load_group((g + 2) % GROUPS)
                if j % 2 and not (last and j > 3):
                    b = it * PER_IT + AHEAD + j // 2
                    for k in range(2):
                        sp.wait_ge(s_pair[k], (b + 1) * (PAIRS // 2))
                    load_key_rows(sp, b + AHEAD, (j // 2) % 2)

        def out_u(mat, it, g, j):
            sp.wait_ge(s_uev[j % 2], it * (KT // 2) + j // 2 + 1)
            sp.dma_start(uT_d[mat, :, j, bass.ds(g * GN, GN)], usb[:, j % 2, :]).then_inc(s_uout[j % 2], 16)

        def load_tile(t, i):
            sp.dma_start(xt[:, i].rearrange("p k r -> p (k r)"),
                         xnT_d[bass.ds(t, 1)].rearrange("o p k r -> (o p) (k r)")).then_inc(s_xt[i], 16)

        def load_units(u, slot):
            for m in range(2):
                sp.dma_start(uu[:, slot, :, m, :], uT_d[m, :, bass.ds((u % GT) * 2, 2), bass.ds((u // GT) % GROUPS * GN, GN)]
                             ).then_inc(s_ut[slot], 16)

        stage2_group(0, 0)
        with sp.Fori(1, GROUPS) as g:
            stage2_group(0, g)
        stage2_group(1, 0)
        with sp.Fori(1, GROUPS - 1) as g:
            stage2_group(1, g)
        stage2_group(1, GROUPS - 1, last=True)
        out_u(1, ITERS - 1, GROUPS - 1, KT - 1)
        for i in range(2):
            sp.wait_ge(s_row[i], 32 * (BLOCKS // 2))
            sp.wait_ge(s_pair[i], BLOCKS * PAIRS // 2)
            sp.wait_ge(s_u[i], Q_BLOCKS)
            sp.wait_ge(s_sq[i], Q_BLOCKS)
            sp.wait_ge(s_uout[i], Q_BLOCKS * 16)
            sp.wait_ge(s_Azero[i], 8 * A_PITCH // P)

        def load_rows_of(w, n, j):
            rows, arrived, _ = row_blocks[n + j]
            sp.dma_start(rows, w[j * P:(j + 1) * P, :]).then_inc(arrived, 16)

        for k in range(2, 5):
            load_rows_of(W, 0, k)
        load_tile(1, 1)
        for k in range(5, KT):
            sp.wait_ge(s_w2h, k - 4)
            sp.wait_ge(s_w2l, k - 4)
            load_rows_of(W, 0, k)
        load_units(0, 0)
        sp.wait_ge(s_w2h, 5)
        sp.wait_ge(s_w2l, 5)
        load_units(1, 1)
        sp.wait_ge(s_w2h, KT)
        sp.wait_ge(s_w2l, KT)
        for j in range(3):
            load_rows_of(Wv, KT, j)
        with sp.Fori(0, TILES // 2) as h:
            for i in range(2):
                sp.wait_ge(s_xth[i], h + 1)
                sp.wait_ge(s_xtl[i], h + 1)
                load_tile((h * 2 + i + 2) % TILES, i)
                for jj in range(2):
                    sp.wait_ge(s_s[jj], h * 2 + i + 1)
                load_units(h * 2 + i + 2, i)
        for i in range(2):
            sp.wait_ge(s_ut[i], 32 * (HALF + 1))
            sp.wait_ge(s_s[i], TILES)
        for j in range(3, KT):
            if j >= 5:
                sp.wait_ge(s_wtr[j % 2 if j == 7 else (j - 5) % 2], KT + (2 if j == 7 else 1))
            load_rows_of(Wv, KT, j)
        sp.wait_ge(s_wtr[0], KT + 2)
        sp.dma_start(bvb[:, :], bv.rearrange("(o n) -> o n", o=1).to_broadcast([P, D])).then_inc(s_bv, 16)
        for i in range(2):
            sp.wait_ge(s_wtr[i], KT + KT // 2)
            sp.wait_ge(s_ut[i], 32 * (HALF + 1))
            sp.wait_ge(s_s[i], TILES)

        def load_x(t, i):
            split_rows(sp, zx[:, i, :], x[bass.ds(t * ROWS, ROWS), :], s_zx[i])

        def load_rows(n):
            f, a = divmod(n % 12, 4)
            if f < 2:
                rows = (w_gate, w_up)[f][a * P:(a + 1) * P, :]
                sp.dma_start(fwb[:, n % 2, :], rows).then_inc(s_fw[n % 2], 16)
            else:
                rows = w_down[2 * a * P:2 * (a + 1) * P, :].rearrange("(b p) n -> p b n", p=P)
                sp.dma_start(fwb[:, n % 2, :].rearrange("p (b n) -> p b n", b=2), rows).then_inc(s_fw[n % 2], 16)

        for i in range(2):
            load_x(i, i)
            load_rows(i)

        def load_A(s, g, i):
            sp.dma_start(Araw[:, i, :], A[bass.ds(s * ROWS, P), bass.ds(g * GN, GN)]).then_inc(s_Ar[i], 16)

        def load_next_A(hh):
            for i in range(2):
                sp.wait_ge(s_hi5[i], hh + 1)
                sp.wait_ge(s_lo5[i], hh + 1)
                load_A(((hh + 1) % HALF) * 2 + i, (hh + 1) // HALF, i)

        def stage4_tile(h, i, chunk):
            t = h * 2 + i
            nxt = (t + 2) % TILES
            sp.wait_ge(s_xth[i], h + HALF + 1)
            sp.wait_ge(s_xtl[i], h + HALF + 1)
            load_tile(nxt, i)
            if chunk is None and isinstance(h, int) and t < 6:
                for a in range(2):
                    sp.wait_ge(s_fabs, 2 * t + a + 1)
                    load_rows(2 * t + a + 2)
            if chunk is not None:
                if chunk + 2 < 12:
                    sp.wait_ge(s_fq16[i], chunk // 2 + 1)
                    load_rows(12 + chunk + 2)
                sp.wait_ge(s_fT[i], chunk // 2 + 1)
                sp.dma_start(wT_d[chunk], fTb[:, i, :]).then_inc(s_fout[i], 16)
            sp.wait_ge(s_z[i], h + 1)
            split_rows(sp, z_d[bass.ds(t * ROWS, ROWS), :], zx[:, i, :], s_xout[i])
            if isinstance(h, int) and t == TILES - 1:
                load_next_A(0)
            sp.wait_ge(s_xout[i], h * 32 + 32)
            load_x(nxt, i)

        for h in range(3):
            for i in range(2):
                stage4_tile(h, i, None)
        for h in range(3, 9):
            for i in range(2):
                stage4_tile(h, i, 2 * (h - 3) + i)
        for i in range(2):
            sp.wait_ge(s_fT[i], 6)
            sp.wait_ge(s_fout[i], 16 * 6)
            sp.wait_ge(s_sc[i], 16 * CHUNKS // 2)
        for i in range(2):
            load_A(i, 0, i)
        for h in range(9, HALF):
            for i in range(2):
                stage4_tile(h, i, None)
        wait_stage4(sp)
        for f in range(3):
            if f:
                load_next_A(f)
            sp.dma_start(wT[:, f], wT_d[4 * f:4 * f + 4].rearrange("c p n -> p c n")).then_inc(s_wT, 16)
        with sp.Fori(3, GROUPS * HALF - 1) as hh:
            load_next_A(hh)
        for i in range(2):
            sp.wait_ge(s_hi5[i], GROUPS * HALF)
            sp.wait_ge(s_lo5[i], GROUPS * HALF)
            sp.wait_ge(s_pe5[i], GROUPS * HALF)
        sp.wait_ge(s_rout, 32 * (GROUPS - 1))

        def load_r(t, i):
            split_rows(sp, rt[:, i, :], r_d[bass.ds(t * ROWS, ROWS), :], s_zx[i])

        for i in range(2):
            load_r(i, i)
        sp.wait_ge(s_rout, 32 * GROUPS)
        with sp.Fori(0, HALF) as h:
            for i in range(2):
                t = h * 2 + i
                sp.wait_ge(s_z[i], HALF + h + 1)
                split_rows(sp, out[bass.ds(t * ROWS, ROWS), :], fin[:, i, :], s_uout[i])
                load_r((t + 2) % TILES, i)
        for i in range(2):
            sp.wait_ge(s_zx[i], ZX_END + 32 * (HALF + 1))
            sp.wait_ge(s_uout[i], Q_BLOCKS * 16 + 32 * HALF)

    @block.gpsimd
    def _(pool):
        pool.memset(wst[:, 0, :], 0.0).then_inc(s_fill, 1)
        pool.memset(ew[:, :], 0.0).then_inc(s_fill, 1)
        for t in (key, away):
            pool.iota(t[:, :], [[0, ROWS_C // 2], [1, 2]], base=A_PITCH - 2, channel_multiplier=A_PITCH,
                      allow_small_or_imprecise_dtypes=True).then_inc(s_fill, 1)
        pool.memset(ident[:, :], 0.0).then_inc(s_const, 1)
        pool.memset(earlier[:, :, :], 1.0).then_inc(s_const, 1)
        pool.memset(eps[:, :], LN_EPS).then_inc(s_const, 1)
        pool.memset(neg_round[:, :], -ROUND).then_inc(s_const, 1)
        pool.wait_ge(s_const, 4)
        pool.affine_select(out=ident[:, :], in_=ident[:, :], compare_op=ALU.not_equal, fill=1.0, base=0,
                           pattern=[[-1, P]], channel_multiplier=1).then_inc(s_const, 1)
        pool.affine_select(out=earlier[:, 1, :], in_=earlier[:, 1, :], compare_op=ALU.is_gt, fill=0.0, base=0,
                           pattern=[[-1, P]], channel_multiplier=1).then_inc(s_const, 1)
        pool.wait_ge(s_const, 6)
        pool.tensor_copy(ident16[:, :], ident[:, :]).then_inc(s_const, 1)

        for i in range(GT):
            pool.wait_ge(s_xTout[i], 16 * GROUPS)
        pool.memset(zeros[:, :], 0.0).then_inc(s_const, 1)
        pool.wait_ge(s_const, 8)
        for i in range(A_PITCH // P):
            if i >= 2:
                pool.wait_ge(s_Azero[i % 2], 16 * (i // 2))
            if i >= 4:
                pool.wait_ge(s_sq[i % 2], (i - 4) // 2 + 1)
            pool.dma_start(A[i * P:(i + 1) * P, :].rearrange("p (r c) -> p r c", r=4),
                           zeros[:, None, :].to_broadcast([P, 4, A_PITCH // 4])).then_inc(s_Azero[i % 2], 16)
        for i in range(2):
            pool.wait_ge(s_Azero[i], 8 * A_PITCH // P)
        cells = A.rearrange("a (b o) -> (a b) o", o=1)
        with pool.Fori(0, BLOCKS // 2) as h:
            for i in range(2):
                b = h * 2 + i
                cols = bass.ds(b * CH_BLOCK, CH_BLOCK)
                pool.wait_ge(s_flags, b + 1)
                pool.tensor_tensor(to_dummy[:, i, :], away[:, cols], dup[:, cols], ALU.mult).then_inc(s_slot, 1)
                pool.tensor_copy(w_slot[:, i, :], wtot[:, cols]).then_inc(s_slot, 1)
                pool.wait_ge(s_slot, b * 4 + 2)
                pool.tensor_tensor(to_dummy[:, i, :], to_dummy[:, i, :], key[:, cols], ALU.add).then_inc(s_slot, 1)
                pool.wait_ge(s_slot, b * 4 + 3)
                pool.sem_inc(s_go, 1)
                pool.tensor_copy(cell_slot[:, i, :], to_dummy[:, i, :]).then_inc(s_slot, 1)
                pool.wait_ge(s_slot, b * 4 + 4)
                for pr in range(PAIRS):
                    for c in range(2):
                        pool.wait_ge(s_sc[c], (b * PAIRS + pr) * 16)
                    pool.sem_inc(s_go, 1)
                    for c in range(2):
                        col = 2 * pr + c
                        pool.indirect_dma_start(cells, bass.IndirectOffsetOnAxis(cell_slot[:, i, col:col + 1], 0),
                                                w_slot[:, i, col:col + 1], None,
                                                compute_op=ALU.add).then_inc(s_sc[c], 16)

        def load_z(g):
            split_rows(pool, zr[:, :, :], z_d[bass.ds(g * GN, GN), :].rearrange("(t r) d -> r t d", r=ROWS), s_zin)

        def store_r(g):
            split_rows(pool, r_d[bass.ds(g * GN, GN), :].rearrange("(t r) d -> r t d", r=ROWS), zr[:, :, :], s_rout)

        wait_stage4(pool)
        pool.wait_ge(s_lo5[1], 5)
        load_z(0)
        with pool.Fori(0, GROUPS - 1) as g:
            for d in range(GT):
                pool.wait_ge(s_r[d], g + 1)
            pool.sem_inc(s_go, 1)
            store_r(g)
            pool.wait_ge(s_rout, g * 32 + 32)
            pool.wait_ge(s_c5, g * GT + GT)
            pool.sem_inc(s_go, 1)
            load_z(g + 1)
        for d in range(GT):
            pool.wait_ge(s_r[d], GROUPS)
        store_r(GROUPS - 1)
        pool.wait_ge(s_rout, 32 * GROUPS)

    @block.scalar
    def _(act):
        act.wait_ge(s_tr0, 1)
        nc.scalar.activation(bdH[:, :, :], by_block(two_banks(0)), ACT.Copy).then_inc(s_ev0, 1)
        for q in range(2):
            act.wait_ge(s_tr0, q + 2)
            nc.scalar.activation(kT_sb[0:CT, 4 * q:4 * q + 4, :], PS[0:CT, 4 + q, :].rearrange("p (b n) -> p b n", b=4),
                                 ACT.Copy).then_inc(s_ev0, 1)
        act.wait_ge(s_ev0, 3)
        for q, dram in ((0, key_d), (1, ew_d)):
            act.dma_start(dram.rearrange("(b c) p -> c b p", c=CT), kT_sb[0:CT, 4 * q:4 * q + 4, :]).then_inc(s_kout, 16)
        act.wait_ge(s_const, 4)
        for g in range(GROUPS):
            cols = slice(g * GT, (g + 1) * GT)
            act.wait_ge(s_st, g * GT + GT)
            nc.scalar.activation(std[0:ROWS, cols], mv[0:ROWS, cols, 1], ACT.Sqrt, bias=eps[0:ROWS, :]).then_inc(s_std, 1)
            for t in range(g * GT, (g + 1) * GT):
                i = t % 2
                act.wait_ge(s_xtr[i], t // 2 + 1)
                if g:
                    act.wait_ge(s_xTout[t % GT], g * 16)
                nc.scalar.activation(XT[:, t % GT], by_block(two_banks(i))[:, :, 0:ROWS], ACT.Copy).then_inc(s_xev[i], 1)

        def high_of_group_tile(n_group, t):
            nc.scalar.activation(xgH[:, bass.ds(n_group % 2, 1), :, t * ROWS:(t + 1) * ROWS]
                                 .rearrange("p o k r -> p (o k) r"), xg[:, t], ACT.Copy).then_inc(s_xgh, 1)

        act.wait_ge(s_xg, 16)
        for t in range(GT):
            high_of_group_tile(0, t)
        act.wait_ge(s_bias, 32)
        act.wait_ge(s_kout, 32)
        for i in range(GT):
            act.wait_ge(s_xTout[i], 16 * GROUPS)

        def high_of_rows(mat, j):
            act.wait_ge(s_wtr[j % 2], mat * (KT // 2) + j // 2 + 1)
            nc.scalar.activation(WH[:, :, j * P:(j + 1) * P], by_block(two_banks(j % 2)), ACT.Copy).then_inc(s_wh[j % 2], 1)
            load_row_block(act, (Wq, Wk, W)[mat + (j + 2) // KT], (j + 2) % KT)

        def evacuate_u(it, j):
            m = it * (KT // 2) + j // 2
            act.wait_ge(s_u[j % 2], m + 1)
            act.wait_ge(s_uout[j % 2], m * 16)
            nc.scalar.activation(usb[:, j % 2, :], PS[:, 6 + j % 2, 0:GN], ACT.Copy).then_inc(s_uev[j % 2], 1)

        def stage2_group(mat, g, own=False, ahead=False):
            it = g + mat * GROUPS
            if own:
                for j in range(2):
                    high_of_rows(mat, j)
            for j in range(KT):
                m = it * (KT // 2) + j // 2
                act.wait_ge(s_q[j % 2], m + 1)
                act.wait_ge(s_u[j % 2], m)
                bias = bqk[:, mat, j:j + 1]
                nc.scalar.activation(qH[:, j % 2, :], PS[:, 4 + j % 2, 0:GN], ACT.Identity, bias=bias)
                nc.scalar.activation(squares[:, j % 2, :], PS[:, 4 + j % 2, 0:GN], ACT.Square, bias=bias,
                                     accum_out=ssq[:, bass.ds(it * KT + j, 1)]).then_inc(s_sq[j % 2], 1)
                if own and j + 2 < KT:
                    high_of_rows(mat, j + 2)
                if ahead:
                    high_of_rows(mat + 1, j)
                if j:
                    evacuate_u(it, j - 1)
                elif not own:
                    evacuate_u(it - 1, KT - 1)
                if j == 0:
                    act.wait_ge(s_xg, it * 16 + 32)
                if j < GT:
                    high_of_group_tile(it + 1, j)

        stage2_group(0, 0, own=True)
        with act.Fori(1, GROUPS - 1) as g:
            stage2_group(0, g)
        stage2_group(0, GROUPS - 1, ahead=True)
        stage2_group(1, 0)
        with act.Fori(1, GROUPS) as g:
            stage2_group(1, g)
        evacuate_u(ITERS - 1, KT - 1)

        def high_of_tile(i, m):
            act.wait_ge(s_xt[i], m * 16 + 16)
            act.wait_ge(s_mm[i], m)
            nc.scalar.activation(xtH[i][:, :, :], xt[:, i], ACT.Copy).then_inc(s_xth[i], 1)

        for i in range(2):
            act.wait_ge(s_pair[i], BLOCKS * PAIRS // 2)
        for k in range(KT):
            rows, arrived, count = row_blocks[k]
            act.wait_ge(arrived, count)
            nc.scalar.activation(WH[:, k, :], rows, ACT.Copy).then_inc(s_w2h, 1)
            if k == 0:
                high_of_tile(0, 0)
        act.wait_ge(s_norm, 2)
        nc.scalar.activation(norms[:, 1, :], PS[:, 7, 0:2], ACT.Sqrt).then_inc(s_norm, 1)
        act.wait_ge(s_norm, 6)
        nc.scalar.activation(norms[:, 4, :], norms[:, 3, :], ACT.Exp, scale=-0.5).then_inc(s_norm, 1)
        act.wait_ge(s_norm, 4)
        act.wait_ge(s_xg, 16 * (ITERS + 1))
        with act.Fori(0, HALF) as h:
            for i in range(2):
                high_of_tile(1 - i, h + i)
                for jj in range(2):
                    if jj == 0:
                        act.wait_ge(s_ut[i], h * 32 + 32)
                    for m in range(2):
                        nc.scalar.activation(uu[:, i, jj, m, :], uu[:, i, jj, m, :], ACT.Exp,
                                             scale=norms[:, 2, m:m + 1]).then_inc(s_exp[jj], 1)
                act.wait_ge(s_mm[i], h + 1)
                nc.scalar.activation(S[0:ROWS, bass.ds(h * 2 + i, 1), :].rearrange("p o n -> p (o n)"),
                                     two_banks(i)[0:ROWS], ACT.Copy).then_inc(s_supev[i], 1)
        for j in range(KT):
            act.wait_ge(s_wtr[j % 2], KT + j // 2 + 1)
            nc.scalar.activation(WH[:, :, j * P:(j + 1) * P], by_block(two_banks(2 + j % 2)), ACT.Copy).then_inc(s_wh[j % 2], 1)
        with act.Fori(0, 3) as h:
            for i in range(2):
                high_of_tile(1 - i, h + HALF + i)
                for a in range(2):
                    act.wait_ge(s_fw[a], (h * 2 + i) * 16 + 16)
                    nc.scalar.activation(fqb[:, a, :], fwb[:, a, :], ACT.Abs,
                                         accum_out=wabs[:, bass.ds((h * 2 + i) * 2 + a, 1)]).then_inc(s_fabs, 1)
        with act.Fori(3, 9) as h:
            for i in range(2):
                high_of_tile(1 - i, h + HALF + i)
                act.wait_ge(s_fr[i], h - 2)
                act.wait_ge(s_ftr[i], h - 3)
                nc.scalar.activation(fqb[:, i, :], fwb[:, i, :], ACT.Identity, bias=neg_round[:, :]).then_inc(s_fq16[i], 1)
                act.wait_ge(s_ftr[i], h - 2)
                act.wait_ge(s_fout[i], (h - 3) * 16)
                nc.scalar.activation(fTb[:, i, :], PS16[:, 6 + i, :], ACT.Copy).then_inc(s_fT[i], 1)
        for i in range(2):
            high_of_tile(1 - i, 9 + HALF + i)
        def high_of_sources(s, i, m):
            act.wait_ge(s_Ar[i], m * 16 + 16)
            act.wait_ge(s_pe5[i], m)
            nc.scalar.activation(AH[i][0:ROWS, :], Araw[0:ROWS, i, :], ACT.Copy)
            nc.scalar.activation(SH[0:ROWS, i, :], S[0:ROWS, bass.ds(s, 1), :].rearrange("p o n -> p (o n)"),
                                 ACT.Copy).then_inc(s_hi5[i], 1)

        def high_of_pair(g, h):
            for i in range(2):
                high_of_sources(h * 2 + i, i, g * HALF + h)

        def deviation(g):
            act.wait_ge(s_rmv, g + 1)
            nc.scalar.activation(std[0:ROWS, 0:GT], group_mv[0:ROWS, :, 1], ACT.Sqrt, bias=eps[0:ROWS, :]).then_inc(s_std, 1)

        def integers(g, d):
            act.wait_ge(s_rq[d % 2], g * (GT // 2) + d // 2 + 1)
            nc.scalar.activation(rq16[0:ROWS, bass.ds(g * GT + d, 1), :].rearrange("p o n -> p (o n)"),
                                 rc[0:ROWS, d % 2, :], ACT.Identity, bias=neg_round[0:ROWS, :]).then_inc(s_rq16[d % 2], 1)

        for i in range(2):
            act.wait_ge(s_mm[i], TILES)
        with act.Fori(0, HALF) as h:
            high_of_pair(0, h)
        with act.Fori(1, GROUPS) as g:
            high_of_pair(g, 0)
            high_of_pair(g, 1)
            deviation(g - 1)
            for d in range(GT):
                high_of_pair(g, 2 + d)
                integers(g - 1, d)
            with act.Fori(2 + GT, HALF) as h:
                high_of_pair(g, h)
        def transposed_x(i, m):
            act.wait_ge(s_rtr[i], m + 1)
            act.wait_ge(s_q[i], Q_BLOCKS + m)
            nc.scalar.activation(rqT[:, i, :, 0:ROWS], by_block(PS16[:, 6, :])[:, :, 0:ROWS], ACT.Copy).then_inc(s_rqT[i], 1)

        def silu_gate(t, i, m):
            act.wait_ge(s_acc[2 * i], GROUPS + m + 1)
            act.wait_ge(s_h[i], m)
            nc.scalar.activation(gate[0:ROWS, i, :], PS[0:ROWS, 2 * i, :], ACT.Silu,
                                 scale=g_back[0:ROWS, bass.ds(t, 1)]).then_inc(s_gate[i], 1)

        def ffn_tile(h, i):
            act.wait_ge(s_hq[i], h + 1)
            act.wait_ge(s_xtr[i], HALF + h)
            nc.scalar.activation(hq16[0:ROWS, i, :], hid[0:ROWS, i, :], ACT.Identity,
                                 bias=neg_round[0:ROWS, :]).then_inc(s_hq16[i], 1)
            silu_gate((h * 2 + i + 1) % TILES, 1 - i, h + i)
            act.wait_ge(s_xtr[i], HALF + h + 1)
            act.wait_ge(s_u[i], Q_BLOCKS + h)
            nc.scalar.activation(hqT[:, i, :, 0:ROWS],
                                 PS16[:, 7, 0:512].rearrange("p (k n) -> p k n", k=4)[:, :, 0:ROWS],
                                 ACT.Copy).then_inc(s_xev[i], 1)
            transposed_x(i, h + 1)

        act.wait_ge(s_fb, 1)
        transposed_x(0, 0)
        silu_gate(0, 0, 0)
        transposed_x(1, 0)
        ffn_tile(0, 0)
        deviation(GROUPS - 1)
        for d in range(1, GT):
            ffn_tile(d // 2, d % 2)
            integers(GROUPS - 1, d - 1)
        integers(GROUPS - 1, GT - 1)
        act.wait_ge(s_fb, 2)
        with act.Fori(GT // 2, HALF) as h:
            for i in range(2):
                ffn_tile(h, i)

    @block.vector
    def _(dve):
        nc.vector.memset(XN[96:P, :, :], 0.0).then_inc(s_pad, 1)
        for h in range(2):
            for c in range(2):
                nc.vector.memset(sel[h * HD:(h + 1) * HD, c:c + 1], float(h == c)).then_inc(s_pad, 1)
        dve.wait_ge(s_fill, 4)
        dve.wait_ge(s_edges, 64)
        nc.vector.scalar_tensor_tensor(key[:, 0:FULL], iedge[:, 0, 0:FULL], float(A_PITCH), iedge[:, 1, 0:FULL],
                                       ALU.mult, ALU.add).then_inc(s_key, 1)
        nc.vector.scalar_tensor_tensor(key[0:TAIL, FULL:FULL + 1], iedge[0:TAIL, 0, FULL:FULL + 1], float(A_PITCH),
                                       iedge[0:TAIL, 1, FULL:FULL + 1], ALU.mult, ALU.add).then_inc(s_key, 1)
        dve.wait_ge(s_key, 2)
        nc.vector.tensor_tensor(away[:, :], away[:, :], key[:, :], ALU.subtract).then_inc(s_key, 1)
        dve.wait_ge(s_ev0, 1)
        nc.vector.tensor_tensor(bdL[:, :, :], by_block(two_banks(0)), bdH[:, :, :].bitcast(F32),
                                ALU.subtract).then_inc(s_key, 1)

        dve.wait_ge(s_pad, 5)
        for g in range(GROUPS):
            dve.wait_ge(s_x[g], 32)
            if g:
                dve.wait_ge(s_st, 4 * g)
            for t in range(GT):
                for c in range(2):
                    nc.vector.bn_stats(stats[0:ROWS, t, c, :], X[0:ROWS, g * GT + t, c * 512:(c + 1) * 512]).then_inc(s_stc, 1)
            dve.wait_ge(s_stc, 8 * (g + 1))
            for t in range(GT):
                nc.vector.bn_aggr(mv[0:ROWS, g * GT + t, :], stats[0:ROWS, t, :, :].rearrange("p c n -> p (c n)")).then_inc(s_st, 1)
            dve.wait_ge(s_std, g + 1)
            nc.vector.reciprocal(rstd[0:ROWS, g * GT:(g + 1) * GT], std[0:ROWS, g * GT:(g + 1) * GT]).then_inc(s_rstd, 1)
            dve.wait_ge(s_rstd, g + 1)
            for t in range(g * GT, (g + 1) * GT):
                i = t % 2
                if t >= 2:
                    dve.wait_ge(s_xtr[i], t // 2)
                nc.vector.tensor_scalar(XN[0:ROWS, i, :], X[0:ROWS, t, :], mv[0:ROWS, t, 0:1], rstd[0:ROWS, t:t + 1],
                                        ALU.subtract, ALU.mult).then_inc(s_xn[i], 1)
        def low_of_group_tile(n_group, t, n):
            dve.wait_ge(s_xgh, n)
            cols = (bass.ds(n_group % 2, 1), slice(None), slice(t * ROWS, (t + 1) * ROWS))
            nc.vector.tensor_tensor(xgL[(slice(None),) + cols].rearrange("p o k r -> p (o k) r"), xg[:, t],
                                    xgH[(slice(None),) + cols].rearrange("p o k r -> p (o k) r").bitcast(F32),
                                    ALU.subtract).then_inc(s_xgl, 1)

        def first_edges():
            dve.wait_ge(s_const, 6)
            dve.wait_ge(s_ew, 32)
            for b in range(AHEAD):
                dve.wait_ge(s_row[b], 32)
                for i in range(PAIRS):
                    edge_pair(dve, b * PAIRS + i, b * (PAIRS // 2) + i // 2, b, i)
                edge_flags(dve, b)

        for t in range(GT):
            low_of_group_tile(0, t, t + 1)

        def low_of_rows(mat, j):
            dve.wait_ge(s_wh[j % 2], mat * (KT // 2) + j // 2 + 1)
            cols = slice(j * P, (j + 1) * P)
            nc.vector.tensor_tensor(WL[:, :, cols], by_block(two_banks(j % 2)), WH[:, :, cols].bitcast(F32),
                                    ALU.subtract).then_inc(s_wl[j % 2], 1)

        def stage2_group(mat, g, own=False, ahead=False):
            it = g + mat * GROUPS
            if own:
                for j in range(2):
                    low_of_rows(mat, j)
                first_edges()
            for j in range(KT):
                m = it * (KT // 2) + j // 2
                dve.wait_ge(s_sq[j % 2], m + 1)
                nc.vector.scalar_tensor_tensor(qL[:, j % 2, :], PS[:, 4 + j % 2, 0:GN], bqk[:, mat, j:j + 1],
                                               qH[:, j % 2, :].bitcast(F32), ALU.add,
                                               ALU.subtract).then_inc(s_ql[j % 2], 1)
                if own and j + 2 < KT:
                    low_of_rows(mat, j + 2)
                if ahead:
                    low_of_rows(mat + 1, j)
                if j < GT:
                    low_of_group_tile(it + 1, j, it * GT + GT + j + 1)
                b = it * PER_IT + AHEAD + j // 2
                if j % 2 == 0:
                    dve.wait_ge(s_row[(j // 2) % 2], (it * (PER_IT // 2) + AHEAD // 2 + j // 4 + 1) * 32)
                for i in range(2):
                    edge_pair(dve, b * PAIRS + (j % 2) * 2 + i, b * (PAIRS // 2) + j % 2, (j // 2) % 2, (j % 2) * 2 + i)
                if j % 2:
                    edge_flags(dve, b)

        stage2_group(0, 0, own=True)
        with dve.Fori(1, GROUPS - 1) as g:
            stage2_group(0, g)
        stage2_group(0, GROUPS - 1, ahead=True)
        stage2_group(1, 0)
        with dve.Fori(1, GROUPS) as g:
            stage2_group(1, g)
        for i in range(2):
            dve.wait_ge(s_u[i], Q_BLOCKS)
        for i in range(2):
            dve.wait_ge(s_sq[i], ITERS * KT // 2)
        nc.vector.tensor_reduce(norms[:, 0, :], ssq[:, :].rearrange("p (m n) -> p m n", m=2), AX.X, ALU.add).then_inc(s_norm, 1)
        def low_of_tile(i, m):
            dve.wait_ge(s_xth[i], m + 1)
            nc.vector.tensor_tensor(xtL[i][:, :, :], xt[:, i], xtH[i][:, :, :].bitcast(F32), ALU.subtract).then_inc(s_xtl[i], 1)

        for k in range(KT):
            dve.wait_ge(s_w2h, k + 1)
            nc.vector.tensor_tensor(WL[:, k, :], row_blocks[k][0], WH[:, k, :].bitcast(F32), ALU.subtract).then_inc(s_w2l, 1)
            if k == 0:
                low_of_tile(0, 0)
        dve.wait_ge(s_norm, 3)
        nc.vector.reciprocal(norms[:, 2, :], norms[:, 1, :]).then_inc(s_norm, 1)
        dve.wait_ge(s_norm, 4)
        nc.vector.tensor_tensor(norms[:, 3, :], PS[:, 7, 0:2], norms[:, 2, :], ALU.mult).then_inc(s_norm, 1)
        dve.wait_ge(s_norm, 5)
        nc.vector.tensor_tensor(norms[:, 3, :], norms[:, 3, :], norms[:, 2, :], ALU.mult).then_inc(s_norm, 1)
        dve.wait_ge(s_norm, 7)
        nc.vector.tensor_scalar(norms[:, 5, :], norms[:, 4, :], HD ** -0.5, None, ALU.mult).then_inc(s_norm, 1)
        dve.wait_ge(s_norm, 8)
        nc.vector.tensor_tensor(norms[:, 6, 0:1], norms[:, 5, 0:1], norms[:, 5, 1:2], ALU.mult).then_inc(s_norm, 1)
        dve.wait_ge(s_norm, 9)
        with dve.Fori(0, HALF) as h:
            for i in range(2):
                u = h * 2 + i
                low_of_tile(1 - i, h + i)
                for jj in range(2):
                    dve.wait_ge(s_exp[jj], u * 2 + 2)
                    nc.vector.scalar_tensor_tensor(uu[:, i, jj, 0, :], uu[:, i, jj, 0, :], norms[:, 6, 0:1], uu[:, i, jj, 1, :],
                                                   ALU.mult, ALU.mult).then_inc(s_phi[jj], 1)
                for jj in range(2):
                    dve.wait_ge(s_s[jj], u + 1)
                    nc.vector.tensor_copy(s_all[0:ROWS, bass.ds((u // GT) * GT, GT), bass.ds(((u % GT) * 2 + jj) * 2, 2)],
                                          PS[0:ROWS, 4 + jj, 0:2 * GT].rearrange("p (d n) -> p d n", n=2)).then_inc(s_scp[jj], 1)
        for j in range(KT):
            dve.wait_ge(s_wh[j % 2], KT + j // 2 + 1)
            cols = slice(j * P, (j + 1) * P)
            nc.vector.tensor_tensor(WL[:, :, cols], by_block(two_banks(2 + j % 2)), WH[:, :, cols].bitcast(F32),
                                    ALU.subtract).then_inc(s_wl[j % 2], 1)
        for jj in range(2):
            dve.wait_ge(s_scp[jj], TILES)
        for jj in range(2):
            dve.wait_ge(s_s[jj], TILES)
            dve.wait_ge(s_ut[jj], 32 * (HALF + 1))
        nc.vector.reciprocal(rs_all[0:ROWS], s_all[0:ROWS]).then_inc(s_rs, 1)
        dve.wait_ge(s_rs, 1)
        dve.wait_ge(s_bv, 16)

        def stage4_tile(h, i):
            t = h * 2 + i
            v = two_banks(i)[0:ROWS]
            v_heads = v.rearrange("p (h n) -> p h n", h=HEADS)
            dve.wait_ge(s_mm[i], h + HALF + 1)
            nc.vector.tensor_tensor(v, v, bvb[0:ROWS, :], ALU.add).then_inc(s_vc, 1)
            for step, sums in enumerate((s_all, rs_all)):
                dve.wait_ge(s_vc, t * 3 + 1 + step)
                nc.vector.tensor_tensor(v_heads, v_heads, sums[0:ROWS, bass.ds(t, 1), :].rearrange("p o n -> p (o n)")[:, :, None]
                                        .to_broadcast([ROWS, HEADS, HD]), ALU.mult).then_inc(s_vc, 1)
            dve.wait_ge(s_vc, t * 3 + 3)
            dve.wait_ge(s_zx[i], h * 32 + 32)
            nc.vector.tensor_tensor(zx[0:ROWS, i, :], v, zx[0:ROWS, i, :], ALU.add).then_inc(s_z[i], 1)

        with dve.Fori(0, 2) as h:
            for i in range(2):
                low_of_tile(1 - i, h + HALF + i)
                stage4_tile(h, i)
        low_of_tile(1, 2 + HALF)
        stage4_tile(2, 0)
        low_of_tile(0, 3 + HALF)
        dve.wait_ge(s_fabs, 12)
        nc.vector.tensor_reduce(wsum[:, :], wabs[:, :].rearrange("p (f a) -> p f a", f=3), AX.X, ALU.add).then_inc(s_fs, 1)
        stage4_tile(2, 1)
        dve.wait_ge(s_ftot, 1)
        nc.vector.tensor_scalar(wq_sc[:, :, 0], PS[:, 4, 0:3], 1.0 / (INNER * D), QUANT_EPS, ALU.mult, ALU.max).then_inc(s_fc, 1)
        dve.wait_ge(s_fc, 1)
        nc.vector.reciprocal(wq_sc[:, :, 1], wq_sc[:, :, 0]).then_inc(s_fc, 1)
        dve.wait_ge(s_fc, 2)
        nc.vector.reciprocal(wq_sc[:, :, 2], wq_sc[:, :, 1]).then_inc(s_fc, 1)
        dve.wait_ge(s_fc, 3)
        with dve.Fori(3, 9) as h:
            for i in range(2):
                low_of_tile(1 - i, h + HALF + i)
                c = h * 2 + i - 6
                dve.wait_ge(s_fw[i], (h - 3) * 16 + 7 * 16)
                nc.vector.tensor_scalar(fwb[:, i, :], fwb[:, i, :], wq_sc[:, bass.ds(c // 4, 1), 1], 1.0,
                                        ALU.mult, ALU.min).then_inc(s_fm, 1)
                dve.wait_ge(s_fm, c + 1)
                nc.vector.tensor_scalar(fwb[:, i, :], fwb[:, i, :], -1.0, ROUND, ALU.max, ALU.add).then_inc(s_fr[i], 1)
                stage4_tile(h, i)
        low_of_tile(1, 9 + HALF)
        stage4_tile(9, 0)
        low_of_tile(0, 10 + HALF)
        def low_of_sources(s, i, m):
            dve.wait_ge(s_hi5[i], m + 1)
            nc.vector.tensor_tensor(AL[i][0:ROWS, :], Araw[0:ROWS, i, :], AH[i][0:ROWS, :].bitcast(F32), ALU.subtract)
            nc.vector.tensor_tensor(SL[0:ROWS, i, :], S[0:ROWS, bass.ds(s, 1), :].rearrange("p o n -> p (o n)"),
                                    SH[0:ROWS, i, :].bitcast(F32), ALU.subtract).then_inc(s_lo5[i], 1)

        def low_of_pair(g, h):
            for i in range(2):
                low_of_sources(h * 2 + i, i, g * HALF + h)

        def add_z(g):
            dve.wait_ge(s_zin, g * 32 + 32)
            for d in ORDER:
                if d != ORDER[-1]:
                    dve.wait_ge(s_acc[d], g + 1)
                else:
                    dve.wait_ge(s_pe5[1], g * HALF + HALF)
                nc.vector.tensor_tensor(zr[0:ROWS, d, :], two_banks(d)[0:ROWS], zr[0:ROWS, d, :], ALU.add).then_inc(s_r[d], 1)

        def row_stats(g, tiles):
            for d in tiles:
                dve.wait_ge(s_r[d], g + 1)
                for c in range(2):
                    nc.vector.bn_stats(stats[0:ROWS, d, c, :], zr[0:ROWS, d, c * 512:(c + 1) * 512]).then_inc(s_rst, 1)

        def row_moments(g):
            dve.wait_ge(s_rst, g * 8 + 8)
            dve.sem_inc(s_go2, 1)
            for d in range(GT):
                last = nc.vector.bn_aggr(group_mv[0:ROWS, d, :], stats[0:ROWS, d, :, :].rearrange("p c n -> p (c n)"))
            last.then_inc(s_rmv, 1)

        def inverse_deviation(g):
            dve.wait_ge(s_std, g + GROUPS + 1)
            nc.vector.reciprocal(rstd[0:ROWS, 0:GT], std[0:ROWS, 0:GT]).then_inc(s_rstd, 1)
            dve.wait_ge(s_rstd, g + GROUPS + 1)

        def quantise_r(g, d):
            i, n = d % 2, (g * GT + d) * 4
            c, back = rc[0:ROWS, i, :], x_back[0:ROWS, bass.ds(g * GT + d, 1)]
            dve.wait_ge(s_rq16[i], g * (GT // 2) + d // 2)
            nc.vector.tensor_scalar(c, zr[0:ROWS, d, :], group_mv[0:ROWS, d, 0:1], rstd[0:ROWS, d:d + 1],
                                    ALU.subtract, ALU.mult).then_inc(s_c5, 1)
            dve.wait_ge(s_c5, g * GT + d + 1)
            nc.vector.tensor_reduce(f_sc[0:ROWS, d:d + 1], c, AX.X, ALU.max, apply_absolute_value=True).then_inc(s_f6, 1)
            dve.wait_ge(s_f6, n + 1)
            nc.vector.tensor_scalar(back, f_sc[0:ROWS, d:d + 1], QUANT_EPS, 1.0 / 127.0, ALU.max, ALU.mult).then_inc(s_f6, 1)
            dve.wait_ge(s_f6, n + 2)
            dve.sem_inc(s_go2, 1)
            nc.vector.reciprocal(f_sc[0:ROWS, d:d + 1], back).then_inc(s_f6, 1)
            dve.wait_ge(s_f6, n + 3)
            nc.vector.tensor_scalar(c, c, f_sc[0:ROWS, d:d + 1], 127.0, ALU.mult, ALU.min).then_inc(s_f6, 1)
            dve.wait_ge(s_f6, n + 4)
            nc.vector.tensor_scalar(c, c, -128.0, ROUND, ALU.max, ALU.add).then_inc(s_rq[i], 1)

        low_of_sources(0, 0, 0)
        stage4_tile(9, 1)
        low_of_sources(1, 1, 0)
        with dve.Fori(1, HALF) as h:
            low_of_pair(0, h)
        with dve.Fori(1, GROUPS) as g:
            low_of_sources(0, 0, g * HALF)
            add_z(g - 1)
            low_of_sources(1, 1, g * HALF)
            row_stats(g - 1, ORDER[:2])
            low_of_sources(2, 0, g * HALF + 1)
            row_stats(g - 1, ORDER[2:])
            row_moments(g - 1)
            low_of_sources(3, 1, g * HALF + 1)
            inverse_deviation(g - 1)
            for d in range(GT):
                quantise_r(g - 1, d)
                low_of_pair(g, 2 + d)
            with dve.Fori(2 + GT, HALF) as h:
                low_of_pair(g, h)
        def scales_back(tiles):
            nc.vector.tensor_scalar(u_back[0:ROWS, tiles], x_back[0:ROWS, tiles], wq_sc[0:ROWS, 1, 2:3], None, ALU.mult)
            nc.vector.tensor_scalar(g_back[0:ROWS, tiles], x_back[0:ROWS, tiles], wq_sc[0:ROWS, 0, 2:3], None,
                                    ALU.mult).then_inc(s_fb, 1)

        def hidden(h, i):
            t = h * 2 + i
            sc, hh = h_sc[0:ROWS, i, :], hid[0:ROWS, i, :]
            n = t * 5
            dve.wait_ge(s_gate[i], h + 1)
            dve.wait_ge(s_q[i], Q_BLOCKS + h + 1)
            dve.wait_ge(s_hq16[i], h)
            nc.vector.scalar_tensor_tensor(hh, PS[0:ROWS, 2 * i + 1, :], u_back[0:ROWS, bass.ds(t, 1)], gate[0:ROWS, i, :],
                                           ALU.mult, ALU.mult).then_inc(s_h[i], 1)
            dve.wait_ge(s_h[i], h + 1)
            nc.vector.tensor_reduce(sc[:, 0:1], hh, AX.X, ALU.max, apply_absolute_value=True).then_inc(s_h6, 1)
            dve.wait_ge(s_h6, n + 1)
            nc.vector.tensor_scalar(sc[:, 0:1], sc[:, 0:1], QUANT_EPS, 1.0 / 127.0, ALU.max, ALU.mult).then_inc(s_h6, 1)
            dve.wait_ge(s_h6, n + 2)
            nc.vector.reciprocal(sc[:, 1:2], sc[:, 0:1]).then_inc(s_h6, 1)
            nc.vector.tensor_tensor(sc[:, 2:3], sc[:, 0:1], wq_sc[0:ROWS, 2, 2:3], ALU.mult).then_inc(s_h6, 1)
            dve.wait_ge(s_h6, n + 4)
            nc.vector.tensor_scalar(hh, hh, sc[:, 1:2], 127.0, ALU.mult, ALU.min).then_inc(s_h6, 1)
            dve.wait_ge(s_h6, n + 5)
            nc.vector.tensor_scalar(hh, hh, -128.0, ROUND, ALU.max, ALU.add).then_inc(s_hq[i], 1)

        def add_down(h, i):
            dve.wait_ge(s_u[i], Q_BLOCKS + h + 1)
            dve.wait_ge(s_uout[i], Q_BLOCKS * 16 + h * 32)
            dve.wait_ge(s_zx[i], ZX_END + h * 32 + 32)
            nc.vector.scalar_tensor_tensor(fin[0:ROWS, i, :], PS[0:ROWS, 4:6, :].rearrange("p b n -> p (b n)"),
                                           h_sc[0:ROWS, i, 2:3], rt[0:ROWS, i, :], ALU.mult, ALU.add).then_inc(s_z[i], 1)

        dve.wait_ge(s_rq[1], (TILES - GT) // 2)
        scales_back(slice(0, TILES - GT))
        add_z(GROUPS - 1)
        dve.wait_ge(s_fb, 1)
        hidden(0, 0)
        row_stats(GROUPS - 1, ORDER)
        row_moments(GROUPS - 1)
        hidden(0, 1)
        inverse_deviation(GROUPS - 1)
        quantise_r(GROUPS - 1, 0)
        add_down(0, 0)
        hidden(1, 0)
        quantise_r(GROUPS - 1, 1)
        add_down(0, 1)
        hidden(1, 1)
        quantise_r(GROUPS - 1, 2)
        add_down(1, 0)
        quantise_r(GROUPS - 1, 3)
        dve.wait_ge(s_rq[1], TILES // 2)
        scales_back(slice(TILES - GT, TILES))
        dve.wait_ge(s_fb, 2)
        with dve.Fori(GT // 2, HALF) as h:
            hidden(h, 0)
            add_down(h - 1, 1)
            hidden(h, 1)
            add_down(h, 0)
        add_down(HALF - 1, 1)

    @block.tensor
    def _(pe):
        def transposes(slot, rows):
            for k in range(KT):
                last = nc.tensor.transpose(by_block(two_banks(slot))[:, k, :], rows[:, k * P:(k + 1) * P], ident[:, :])
            return last

        pe.wait_ge(s_const, 6)
        pe.wait_ge(s_bd, 32)
        transposes(0, wst[:, 0, :]).then_inc(s_tr0, 1)
        pe.wait_ge(s_key, 2)
        pe.wait_ge(s_ew, 32)
        for q, t in enumerate((key, ew)):
            for b in range(4):
                last = nc.tensor.transpose(PS[0:CT, 4 + q, b * P:(b + 1) * P], t[:, b * CT:(b + 1) * CT], ident[:, :])
            last.then_inc(s_tr0, 1)
        pe.wait_ge(s_key, 4)
        with pe.Fori(0, TILES // 2) as h:
            for i in range(2):
                pe.wait_ge(s_xn[i], h + 1)
                pe.wait_ge(s_xev[i], h)
                transposes(i, XN[:, i, :]).then_inc(s_xtr[i], 1)
        for i in range(2):
            pe.wait_ge(s_xev[i], TILES // 2)
        pe.wait_ge(s_ev0, 3)

        def transpose_rows(mat, j):
            m = mat * (KT // 2) + j // 2
            pe.wait_ge(s_wst[j % 2], m * 16 + 16)
            pe.wait_ge(s_wh[j % 2], m)
            pe.wait_ge(s_wl[j % 2], m)
            transposes(j % 2, wst[:, j % 2, :]).then_inc(s_wtr[j % 2], 1)

        def maps(it, j):
            m = it * (KT // 2) + j // 2
            pe.wait_ge(s_ql[j % 2], m + 1)
            pe.wait_ge(s_uev[j % 2], m)
            product3(PS[:, 6 + j % 2, 0:GN], bdH[:, j, :], bdL[:, j, :], qH[:, j % 2, :], qL[:, j % 2, :],
                     True, True).then_inc(s_u[j % 2], 1)

        def stage2_group(mat, g, own=False, ahead=False):
            it = g + mat * GROUPS
            if own:
                for j in range(2):
                    transpose_rows(mat, j)
            pe.wait_ge(s_xgl, it * GT + GT)
            for j in range(KT):
                m = it * (KT // 2) + j // 2
                if own or mat and isinstance(g, int) and g == 0:
                    pe.wait_ge(s_wl[j % 2], mat * (KT // 2) + j // 2 + 1)
                pe.wait_ge(s_sq[j % 2], m)
                pe.wait_ge(s_ql[j % 2], m)
                cols = slice(j * P, (j + 1) * P)
                for k in range(KT):
                    rh, rl = (b[:, bass.ds(it % 2, 1), k, :].rearrange("p o n -> p (o n)") for b in (xgH, xgL))
                    last = product3(PS[:, 4 + j % 2, 0:GN], WH[:, k, cols], WL[:, k, cols], rh, rl,
                                    k == 0, k == KT - 1)
                last.then_inc(s_q[j % 2], 1)
                if own and j + 2 < KT:
                    transpose_rows(mat, j + 2)
                if ahead:
                    transpose_rows(mat + 1, j)
                if j:
                    maps(it, j - 1)
                elif not own:
                    maps(it - 1, KT - 1)

        stage2_group(0, 0, own=True)
        with pe.Fori(1, GROUPS - 1) as g:
            stage2_group(0, g)
        stage2_group(0, GROUPS - 1, ahead=True)
        stage2_group(1, 0)
        with pe.Fori(1, GROUPS) as g:
            stage2_group(1, g)
        maps(ITERS - 1, KT - 1)
        pe.wait_ge(s_norm, 1)
        pe.wait_ge(s_uev[1], Q_BLOCKS)
        nc.tensor.matmul(PS[:, 7, 0:2], earlier[:, 0, :], norms[:, 0, :], start=True, stop=True).then_inc(s_norm, 1)

        def tile_products(i, ready=None, half_ready=None):
            order = [(k, c) for k in range(KT) for c in range(2)]
            if half_ready:
                order = [(k, c) for c in range(2) for k in range(KT)]
            for k, c in order:
                if ready is not None and c == 0:
                    pe.wait_ge(ready, k + 1)
                if half_ready and k == 0:
                    half_ready(c)
                cols = slice(c * 512, (c + 1) * 512)
                last = product3(PS[0:ROWS, 2 * i + c, :], xtH[i][:, k, :], xtL[i][:, k, :], WH[:, k, cols],
                                WL[:, k, cols], k == 0, k == KT - 1)
            last.then_inc(s_mm[i], 1)

        pe.wait_ge(s_pad, 5)

        def map_sums(i, u):
            for jj in range(2):
                pe.wait_ge(s_phi[jj], u + 1)
                pe.wait_ge(s_scp[jj], u)
                for d in range(GT):
                    last = nc.tensor.matmul(PS[0:ROWS, 4 + jj, 2 * d:2 * d + 2], uu[:, i, jj, 0, d * ROWS:(d + 1) * ROWS],
                                            sel[:, :], start=True, stop=True)
                last.then_inc(s_s[jj], 1)

        for i in range(2):
            pe.wait_ge(s_xtl[i], 1)
            tile_products(i, ready=s_w2l if i == 0 else None)
            map_sums(i, i)
        with pe.Fori(1, HALF) as h:
            for i in range(2):
                pe.wait_ge(s_xtl[i], h + 1)
                pe.wait_ge(s_supev[i], h)
                tile_products(i)
                map_sums(i, h * 2 + i)

        def transpose_rows_v(j):
            rows, arrived, count = row_blocks[KT + j]
            pe.wait_ge(arrived, count)
            pe.wait_ge(s_wl[j % 2], KT + j // 2)
            transposes(2 + j % 2, rows).then_inc(s_wtr[j % 2], 1)

        def rows_of_half(c):
            for j in range(4 * c + 2 if c else 0, 4 * c + 6 if not c else KT):
                transpose_rows_v(j)
            for k in range(2):
                pe.wait_ge(s_wl[k], KT + 2 * c + 2)

        for jj in range(2):
            pe.wait_ge(s_scp[jj], TILES)
        for i in range(2):
            pe.wait_ge(s_xtl[i], HALF + 1)
            pe.wait_ge(s_supev[i], HALF)
            tile_products(i, half_ready=rows_of_half if i == 0 else None)
        with pe.Fori(1, 3) as h:
            for i in range(2):
                pe.wait_ge(s_xtl[i], h + HALF + 1)
                pe.wait_ge(s_z[i], h)
                tile_products(i)
        pe.wait_ge(s_fs, 1)
        nc.tensor.matmul(PS[:, 4, 0:3], earlier[:, 0, :], wsum[:, :], start=True, stop=True).then_inc(s_ftot, 1)
        pe.wait_ge(s_const, 7)
        with pe.Fori(3, 9) as h:
            for i in range(2):
                pe.wait_ge(s_xtl[i], h + HALF + 1)
                pe.wait_ge(s_z[i], h)
                tile_products(i)
                pe.wait_ge(s_fq16[i], h - 2)
                pe.wait_ge(s_fT[i], h - 3)
                for e in range(8):
                    last = nc.tensor.transpose(PS16[:, 6 + i, e * P:(e + 1) * P], fqb[:, i, e * P:(e + 1) * P], ident16[:, :])
                last.then_inc(s_ftr[i], 1)
        for i in range(2):
            pe.wait_ge(s_xtl[i], 9 + HALF + 1)
            pe.wait_ge(s_z[i], 9)
            tile_products(i)
        pe.wait_ge(s_z[0], HALF)
        for i in range(2):
            pe.wait_ge(s_fT[i], 6)
        pe.wait_ge(s_fc, 3)

        def sources(g, i, m, first, last_one):
            pe.wait_ge(s_lo5[i], m + 1)
            for d in ORDER:
                if first:
                    pe.wait_ge(s_r[d], g)
                    if d == 1:
                        pe.wait_ge(s_z[1], HALF)
                rows = slice(d * ROWS, (d + 1) * ROWS)
                for c in range(2):
                    cols = slice(c * 512, (c + 1) * 512)
                    last = product3(PS[0:ROWS, 2 * d + c, :], AH[i][0:ROWS, rows], AL[i][0:ROWS, rows],
                                    SH[0:ROWS, i, cols], SL[0:ROWS, i, cols], first, last_one)
                if last_one and d != ORDER[-1]:
                    last.then_inc(s_acc[d], 1)
            last.then_inc(s_pe5[i], 1)

        with pe.Fori(0, GROUPS) as g:
            for i in range(2):
                sources(g, i, g * HALF, i == 0, False)
            with pe.Fori(1, HALF - 1) as h:
                for i in range(2):
                    sources(g, i, g * HALF + h, False, False)
            for i in range(2):
                sources(g, i, g * HALF + HALF - 1, False, i == 1)
        pe.wait_ge(s_wT, 48)

        def transpose_x(t, i, m):
            if i == 0:
                pe.wait_ge(s_rqT[1], m)
            else:
                pe.wait_ge(s_rqT[0], m + 1)
            for k in range(KT):
                last = nc.tensor.transpose(PS16[:, 6, k * P:k * P + ROWS],
                                           rq16[0:ROWS, bass.ds(t, 1), k * P:(k + 1) * P].rearrange("p o n -> p (o n)"),
                                           ident16[0:ROWS, 0:ROWS])
            last.then_inc(s_rtr[i], 1)

        def down_blocks(c, k):
            return wT[:, 2, 2 * c:2 * c + 2, :].rearrange("p a (b n) -> p (a b) n", b=2)[:, :, k * P:(k + 1) * P]

        def gate_up(i, m):
            pe.wait_ge(s_rqT[i], m + 1)
            pe.wait_ge(s_h[i], m)
            for c in range(2):
                for k in range(KT):
                    last = nc.tensor.matmul(PS[0:ROWS, 2 * i + c, :], rqT[:, i, k, 0:ROWS], wT[:, c, :, k * P:(k + 1) * P],
                                            start=k == 0, stop=k == KT - 1)
                if c == 0:
                    last.then_inc(s_acc[2 * i], 1)
            last.then_inc(s_q[i], 1)

        def ffn_tile(h, i):
            gate_up(1 - i, h + i)
            pe.wait_ge(s_hq16[i], h + 1)
            if i == 0:
                pe.wait_ge(s_xev[1], HALF + h)
            else:
                pe.wait_ge(s_xev[0], HALF + h + 1)
            for k in range(INNER // P):
                last = nc.tensor.transpose(PS16[:, 7, k * P:k * P + ROWS], hq16[0:ROWS, i, k * P:(k + 1) * P],
                                           ident16[0:ROWS, 0:ROWS])
            last.then_inc(s_xtr[i], 1)
            transpose_x((h * 2 + i + 2) % TILES, i, h + 1)
            pe.wait_ge(s_xev[i], HALF + h + 1)
            if i == 0:
                pe.wait_ge(s_z[1], HALF + h)
            else:
                pe.wait_ge(s_z[0], HALF + h + 1)
            for c in range(2):
                for k in range(INNER // P):
                    last = nc.tensor.matmul(PS[0:ROWS, 4 + c, :], hqT[:, i, k, 0:ROWS], down_blocks(c, k),
                                            start=k == 0, stop=k == INNER // P - 1)
            last.then_inc(s_u[i], 1)

        for i in range(2):
            pe.wait_ge(s_rq16[i], (TILES - GT) // 2)
        for d in (0, 3):
            pe.wait_ge(s_r[d], GROUPS)
        transpose_x(0, 0, 0)
        gate_up(0, 0)
        transpose_x(1, 1, 0)
        for d in (1, 2):
            pe.wait_ge(s_r[d], GROUPS)
        for d in range(GT):
            ffn_tile(d // 2, d % 2)
        for i in range(2):
            pe.wait_ge(s_rq16[i], TILES // 2)
        with pe.Fori(GT // 2, HALF) as h:
            for i in range(2):
                ffn_tile(h, i)

    block_cm.__exit__(None, None, None)


_INS = ['x', 'src', 'dst', 'edge_weight', 'L0_gnn_W', 'L0_mix_Wq', 'L0_mix_bq', 'L0_mix_Wk', 'L0_mix_bk',
        'L0_mix_Wv', 'L0_mix_bv', 'L0_mix_weights', 'L0_ffn_w_gate', 'L0_ffn_w_up', 'L0_ffn_w_down']


def kernel(**inputs):
    import concourse.bacc as bacc
    from concourse.bass_utils import run_bass_kernel_spmd

    nc = bacc.Bacc("TRN2", target_bir_lowering=False, num_devices=1)
    arrays, args = {}, []
    for name in _INS:
        a = np.ascontiguousarray(inputs[name])
        arrays["in_" + name] = a
        args.append(nc.dram_tensor("in_" + name, a.shape, mybir.dt.from_np(a.dtype), kind="ExternalInput").ap())
    args.append(nc.dram_tensor("out_r", (NODES, D), F32, kind="ExternalOutput").ap())
    layer_kernel(nc, *args)
    r = run_bass_kernel_spmd(nc, [arrays], core_ids=[0])
    return r.results[0]["out_r"]
```
